# Optimizing a Trainium2 kernel written in Bass

```python
import numpy as np
import jax
import jax.numpy as jnp

def _softmax(x, axis=-1):
    return jax.nn.softmax(x, axis=axis)

def _gelu(x):
    return jax.nn.gelu(x, approximate=True)

def _silu(x):
    return jax.nn.silu(x)

def _sigmoid(x):
    return jax.nn.sigmoid(x)

def _layernorm(x, axis=-1, eps=1e-05):
    m = jnp.mean(x, axis=axis, keepdims=True)
    v = jnp.var(x, axis=axis, keepdims=True)
    return (x - m) / jnp.sqrt(v + eps)

def _scatter_add(tgt, idx, src, axis=0):
    return tgt.at[idx].add(src)

def _segment_sum(src, seg, n):
    return jax.ops.segment_sum(src, seg, n)
kernel_name = 'mk_gnn_resnorm_d2_gnn_r8_3890a3'

def setup_inputs(seed: int=0):
    np.random.seed(seed)
    _w = jnp.asarray

    def _rec_inputs():
        import jax
        import jax.numpy as jnp
        _gk = jax.random.key(seed)
        x = -0.0005121 + 1.001 * jax.random.normal(jax.random.fold_in(_gk, 1), (6250, 64), jnp.float32)
        src = jax.random.randint(jax.random.fold_in(_gk, 2), (200000,), 0, 6250, jnp.int32)
        dst = jax.random.randint(jax.random.fold_in(_gk, 3), (200000,), 0, 6250, jnp.int32)
        _o = jnp.argsort(dst, stable=True)
        src = src[_o]
        dst = dst[_o]
        edge_attr_16 = 0.000254156 + 0.999948 * jax.random.normal(jax.random.fold_in(_gk, 12), (200000, 16), jnp.float32)
        edge_type_8 = jax.random.randint(jax.random.fold_in(_gk, 14), (200000,), 0, 8, jnp.int32)
        return (x, src, dst, edge_attr_16, edge_type_8)
    x, src, dst, edge_attr_16, edge_type_8 = _rec_inputs()

    def _L0_gnn_setup():
        import jax, jax.numpy as jnp
        import numpy as np
        N = 6250
        E = 100000
        D = 64
        EDGE_DIM = 16
        L = 3
        MSG_IN = 2 * D + EDGE_DIM
        UPD_IN = D + D
        key = jax.random.key(seed)
        ks = jax.random.split(key, 8)
        x = jax.random.normal(ks[0], (N, D), dtype=jnp.float32)
        edge_index = jax.random.randint(ks[1], (2, E), 0, N, dtype=jnp.int64)
        edge_attr = jax.random.normal(ks[2], (E, EDGE_DIM), dtype=jnp.float32)
        sc_m = 1.0 / np.sqrt(MSG_IN)
        sc_u = 1.0 / np.sqrt(UPD_IN)
        msg_w = jax.random.uniform(ks[3], (L, MSG_IN, D), jnp.float32, -sc_m, sc_m)
        msg_b = jax.random.uniform(ks[4], (L, D), jnp.float32, -sc_m, sc_m)
        upd_w = jax.random.uniform(ks[5], (L, UPD_IN, D), jnp.float32, -sc_u, sc_u)
        upd_b = jax.random.uniform(ks[6], (L, D), jnp.float32, -sc_u, sc_u)
        return {'x': x, 'edge_index': edge_index, 'edge_attr': edge_attr, 'msg_w': msg_w, 'msg_b': msg_b, 'upd_w': upd_w, 'upd_b': upd_b}
    _L0_gnn_all = _L0_gnn_setup()
    _L0_gnn_in = {k: v for k, v in _L0_gnn_all.items() if k in ('msg_w', 'msg_b', 'upd_w', 'upd_b')}
    del _L0_gnn_all

    def _L1_gnn_setup():
        import jax, jax.numpy as jnp
        import numpy as np
        N_NODES = 12500
        N_EDGES = 150000
        N_RELS = 8
        N_BASES = 4
        DIM = 64

        def _rgcn_layer(h, src, dst, etype, bases, coef, wself, bias):
            W = jnp.einsum('rb,bio->rio', coef, bases)
            hproj = jnp.einsum('ni,rio->rno', h, W)
            msgs = hproj[etype, src]
            agg = jax.ops.segment_sum(msgs, dst, num_segments=h.shape[0])
            return agg + h @ wself + bias
        key = jax.random.key(seed)
        ks = jax.random.split(key, 12)
        xav = np.sqrt(2.0) * np.sqrt(6.0 / (N_NODES + DIM))
        return {'src': jax.random.randint(ks[0], (N_EDGES,), 0, N_NODES), 'dst': jax.random.randint(ks[1], (N_EDGES,), 0, N_NODES), 'etype': jax.random.randint(ks[2], (N_EDGES,), 0, N_RELS), 'emb': jax.random.uniform(ks[3], (N_NODES, DIM), jnp.float32, -xav, xav), 'bases1': jax.random.normal(ks[4], (N_BASES, DIM, DIM), jnp.float32) * 0.05, 'coef1': jax.random.normal(ks[5], (N_RELS, N_BASES), jnp.float32) * 0.3, 'wself1': jax.random.normal(ks[6], (DIM, DIM), jnp.float32) * 0.05, 'bias1': jnp.zeros((DIM,), jnp.float32), 'bases2': jax.random.normal(ks[7], (N_BASES, DIM, DIM), jnp.float32) * 0.05, 'coef2': jax.random.normal(ks[8], (N_RELS, N_BASES), jnp.float32) * 0.3, 'wself2': jax.random.normal(ks[9], (DIM, DIM), jnp.float32) * 0.05, 'bias2': jnp.zeros((DIM,), jnp.float32)}
    _L1_gnn_all = _L1_gnn_setup()
    _L1_gnn_in = {k: v for k, v in _L1_gnn_all.items() if k in ('bases1', 'coef1', 'wself1', 'bias1', 'bases2', 'coef2', 'wself2', 'bias2')}
    del _L1_gnn_all
    return {'x': x, 'src': src, 'dst': dst, 'edge_attr_16': edge_attr_16, 'edge_type_8': edge_type_8, 'L0_gnn_msg_w': _L0_gnn_in['msg_w'], 'L0_gnn_msg_b': _L0_gnn_in['msg_b'], 'L0_gnn_upd_w': _L0_gnn_in['upd_w'], 'L0_gnn_upd_b': _L0_gnn_in['upd_b'], 'L1_gnn_bases1': _L1_gnn_in['bases1'], 'L1_gnn_coef1': _L1_gnn_in['coef1'], 'L1_gnn_wself1': _L1_gnn_in['wself1'], 'L1_gnn_bias1': _L1_gnn_in['bias1'], 'L1_gnn_bases2': _L1_gnn_in['bases2'], 'L1_gnn_coef2': _L1_gnn_in['coef2'], 'L1_gnn_wself2': _L1_gnn_in['wself2'], 'L1_gnn_bias2': _L1_gnn_in['bias2']}

def reference(x, src, dst, edge_attr_16, edge_type_8, L0_gnn_msg_w, L0_gnn_msg_b, L0_gnn_upd_w, L0_gnn_upd_b, L1_gnn_bases1, L1_gnn_coef1, L1_gnn_wself1, L1_gnn_bias1, L1_gnn_bases2, L1_gnn_coef2, L1_gnn_wself2, L1_gnn_bias2):
    import jax
    import jax.numpy as jnp

    def _L0_gnn_ref(x, edge_index, edge_attr, msg_w, msg_b, upd_w, upd_b):
        import jax, jax.numpy as jnp
        import numpy as np
        N = 6250
        E = 100000
        D = 64
        EDGE_DIM = 16
        L = 3
        MSG_IN = 2 * D + EDGE_DIM
        UPD_IN = D + D
        src = edge_index[0]
        dst = edge_index[1]
        n = x.shape[0]
        num_layers = msg_w.shape[0]
        for l in range(num_layers):
            x_i = x[dst]
            x_j = x[src]
            m_in = jnp.concatenate([x_i, x_j, edge_attr], axis=1)
            m = jax.nn.relu(m_in @ msg_w[l] + msg_b[l])
            agg = jax.ops.segment_sum(m, dst, num_segments=n)
            u_in = jnp.concatenate([x, agg], axis=1)
            x = jax.nn.relu(u_in @ upd_w[l] + upd_b[l])
        return x

    def _L1_gnn_ref(src, dst, etype, emb, bases1, coef1, wself1, bias1, bases2, coef2, wself2, bias2):
        import jax, jax.numpy as jnp
        import numpy as np
        N_NODES = 12500
        N_EDGES = 150000
        N_RELS = 8
        N_BASES = 4
        DIM = 64

        def _rgcn_layer(h, src, dst, etype, bases, coef, wself, bias):
            W = jnp.einsum('rb,bio->rio', coef, bases)
            hproj = jnp.einsum('ni,rio->rno', h, W)
            msgs = hproj[etype, src]
            agg = jax.ops.segment_sum(msgs, dst, num_segments=h.shape[0])
            return agg + h @ wself + bias
        h1 = _rgcn_layer(emb, src, dst, etype, bases1, coef1, wself1, bias1)
        h2 = _rgcn_layer(h1, src, dst, etype, bases2, coef2, wself2, bias2)
        return h2
    edge_index = jnp.stack([src, dst])
    x = _layernorm(x + _L0_gnn_ref(x, edge_index, edge_attr_16, L0_gnn_msg_w, L0_gnn_msg_b, L0_gnn_upd_w, L0_gnn_upd_b), axis=-1)
    x = _layernorm(x + _L1_gnn_ref(src, dst, edge_type_8, x, L1_gnn_bases1, L1_gnn_coef1, L1_gnn_wself1, L1_gnn_bias1, L1_gnn_bases2, L1_gnn_coef2, L1_gnn_wself2, L1_gnn_bias2), axis=-1)
    return x

_drawn_inputs = setup_inputs


def setup_inputs(seed=0):
    import zlib

    import numpy as np

    out = dict(_drawn_inputs(seed))
    spreads = {'L1_gnn_bias1': (0.0, 0.1), 'L1_gnn_bias2': (0.0, 0.386)}
    factors = {'edge_attr_16': 3.088, 'L0_gnn_upd_b': 4.786}
    for name, (base, spread) in spreads.items():
        noise = np.random.default_rng([zlib.crc32(name.encode()), seed]).standard_normal(out[name].shape)
        drawn = base * np.exp(spread * noise) if base else spread * noise
        out[name] = jnp.asarray(drawn.astype(out[name].dtype))
    for name, factor in factors.items():
        out[name] = (out[name] * factor).astype(out[name].dtype)
    return out
```

```python
import concourse.bass as bass
from concourse import mybir
from contextlib import ExitStack

F32 = mybir.dt.float32
BF16 = mybir.dt.bfloat16
I32 = mybir.dt.int32
ALU = mybir.AluOpType
ACT = mybir.ActivationFunctionType
AX = mybir.AxisListType

P = 128
D = 64
TILES = 8
CHUNK = P * TILES
GROUP = 7
SPLIT = 4
EPS = 1e-5


def gnn_kernel(nc, xT, x_rows, src, dst, etype, dst_rows, edge_attr,
               msg_w, msg_b, upd_w, upd_b,
               bases1, coef1, wself1, bias1, bases2, coef2, wself2, bias2, out):
    N = out.shape[0]
    NP = xT.shape[1]
    NW = NP // P
    NG = NW // GROUP
    NCH = edge_attr.shape[0]
    NE = edge_attr.shape[1] // TILES
    LAYERS = msg_w.shape[0]
    RLAYERS = 2
    NB, NR = coef1.shape[1], coef1.shape[0]
    PAIRS = NCH // 2
    GN = GROUP * P
    HALF = [(0, SPLIT), (SPLIT, GROUP)]
    LAG = 3
    LATE = 3 + LAYERS + 4 * RLAYERS
    LOADED = 16 * (4 + 3 * LAYERS)
    ds = bass.ds

    with ExitStack() as ctx:
        def sb(name, shape, dt):
            return ctx.enter_context(nc.sbuf_tensor(name, shape, dt))

        def pb(name, shape, dt=F32):
            return ctx.enter_context(nc.psum_tensor(name, shape, dt))

        def sem(name):
            return ctx.enter_context(nc.semaphore(name))

        msg_table = nc.dram_tensor("msg_table", [NP, D], F32).ap()
        rel_table = nc.dram_tensor("rel_table", [NP * NR, D], F32).ap()
        range_dram = nc.dram_tensor("range_dram", [NCH, 2], I32).ap()
        base_dram = nc.dram_tensor("base_dram", [NCH], F32).ap()

        src_sb = sb("src_sb", [P, NCH * TILES], I32)
        rel_sb = sb("rel_sb", [P, NCH * TILES], I32)
        dst_sb = sb("dst_sb", [P, NCH * TILES], I32)
        dst_rel = sb("dst_rel", [P, NCH * TILES], F32)
        base_bc = sb("base_bc", [P, NCH], F32)
        extreme = sb("extreme", [PAIRS, 2, 2], I32)
        window_range = sb("window_range", [PAIRS, 2, 2], I32)
        window_base = sb("window_base", [PAIRS, 2], F32)
        range_row = sb("range_row", [1, 2 * NCH], I32)
        node_id = sb("node_id", [P, NP], I32)
        col_id = sb("col_id", [P, P], I32)
        ident_f = sb("ident_f", [P, P], F32)
        ident_b = sb("ident_b", [P, P], BF16)
        eps_col = sb("eps_col", [P, 1], F32)

        xaT = sb("xaT", [P, NP], F32)
        a3 = sb("a3", [P, NW, 3 * D], BF16)
        b_rows = sb("b_rows", [P, NW, D], F32)
        agg = sb("agg", [P, NW, D], F32)
        xres = sb("xres", [P, NW, D], F32)

        w_ij_all = sb("w_ij_all", [D, LAYERS, 2 * D], F32)
        w_e_diag = sb("w_e_diag", [TILES * NE, LAYERS, TILES * D], F32)
        b_msg = sb("b_msg", [1, LAYERS, GROUP, D], F32)
        ones = sb("ones", [1, P], F32)
        w_upd_all = sb("w_upd_all", [P, LAYERS, D], F32)
        b_upd_all = sb("b_upd_all", [D, LAYERS], F32)
        w_ij = sb("w_ij", [D, 2 * D], F32)
        w_upd = sb("w_upd", [P, D], F32)
        b_upd = sb("b_upd", [D, 1], F32)
        bases = sb("bases", [D, RLAYERS, NB, D], F32)
        coef = sb("coef", [D, RLAYERS, NR, NB], F32)
        w_rel = sb("w_rel", [D, RLAYERS, NR * D + D], F32)
        w_tmp = sb("w_tmp", [D, NR, D], F32)
        bias_bc = sb("bias_bc", [P, RLAYERS, D], F32)

        idx = [sb(f"idx{q}", [P, TILES], I32) for q in range(2)]
        attr = [sb(f"attr{q}", [TILES * NE, P], F32) for q in range(2)]
        gath = [sb(f"gath{q}", [P, TILES, D], F32) for q in range(2)]
        hot = [sb(f"hot{q}", [P, TILES, P], BF16) for q in range(2)]
        hotT = sb("hotT", [P, TILES, P], BF16)
        x_hotA = sb("x_hotA", [P, TILES, P], BF16)
        x_hotT = sb("x_hotT", [P, TILES, P], BF16)
        x_hotB = sb("x_hotB", [P, TILES, P], BF16)
        m3 = [sb(f"m3_{q}", [P, TILES, 3 * D], BF16) for q in range(2)]
        part = sb("part", [P, D], F32)
        x_part = sb("x_part", [P, D], F32)

        stage_T = sb("stage_T", [D, GN], F32)
        stage_rows = sb("stage_rows", [P, GROUP, D], F32)
        a_rest = sb("a_rest", [P, GROUP, D], F32)
        rel_buffer = sb("rel_buffer", [P, GROUP, NR * D], F32)
        rel_rows = [rel_buffer[:, k, :] for k in range(GROUP)]
        chunk_dst = rel_buffer[0:PAIRS, :, :].rearrange("p k d -> p (k d)")[:, 0:2 * CHUNK].bitcast(I32) \
            .rearrange("p (a e) -> p a e", a=2)
        mean = sb("mean", [P, NW], F32)
        var = sb("var", [P, NW], F32)
        rstd = sb("rstd", [P, NW], F32)
        newton = sb("newton", [P, NW], F32)

        hotT_ps = pb("hotT_ps", [P, TILES, P], BF16)
        x_hotT_ps = pb("x_hotT_ps", [P, TILES, P], BF16)
        pre = [pb(f"pre{q}", [P, TILES * D]) for q in range(2)]
        sums = [pb(f"sums{q}", [P, TILES * D]) for q in range(2)]
        x_sums = pb("x_sums", [P, TILES * D])
        col_ps = pb("col_ps", [P, P])
        a_ps = hotT_ps[:, :, :].rearrange("p a b -> p (a b)").bitcast(F32)
        rows_T = [hotT_ps[:, :, :].rearrange("p a b -> p (a b)").bitcast(F32),
                  x_hotT_ps[:, :, :].rearrange("p a b -> p (a b)").bitcast(F32)]
        rel_ps = [pre[0], pre[1], x_sums]

        loaded = sem("loaded")
        late_loaded = sem("late_loaded")
        diag_loaded = sem("diag_loaded")
        range_made = sem("range_made")
        range_stored = sem("range_stored")
        range_loaded = sem("range_loaded")
        const_pool = sem("const_pool")
        setup_dve = sem("setup_dve")

        def chunk_sems(k):
            names = ["hot_built", "z_done", "hi_done", "rest_done", "mid_done", "lo_done", "sums_done",
                     "part_done", "agg_added", "hotT_done", "hotT_copied", "pre_done",
                     "xa_built", "xa_T", "xa_copied", "xb_built", "xb_sums", "xb_part", "xb_added"]
            s = {n: sem(f"{k}_{n}") for n in names}
            for n in ["idx_loaded", "attr_loaded", "gathered"]:
                s[n] = [sem(f"{k}_{n}{q}") for q in range(2)]
            return s

        M = chunk_sems("msg")
        R = chunk_sems("rel")
        agg_zeroed = sem("agg_zeroed")
        xT_staged = sem("xT_staged")
        b_done = sem("b_done")
        ab_done = sem("ab_done")
        b_copied = sem("b_copied")
        a_hi = sem("a_hi")
        a_rested = sem("a_rested")
        a_mid = sem("a_mid")
        a_lo = sem("a_lo")
        x_kept = sem("x_kept")
        msg_stored = sem("msg_stored")
        weights_set = sem("weights_set")
        agg_staged = sem("agg_staged")
        aggT_done = sem("aggT_done")
        aggT_copied = sem("aggT_copied")
        upd_done = sem("upd_done")
        x_updated = sem("x_updated")
        x3_rows = sem("x3_rows")
        x3_added = sem("x3_added")
        norm = sem("norm")
        rel_weights = sem("rel_weights")
        var_done = sem("var_done")
        std_done = sem("std_done")
        h_staged = sem("h_staged")
        hT_done = sem("hT_done")
        hT_copied = sem("hT_copied")
        rel_done = sem("rel_done")
        rel_copied = sem("rel_copied")
        rel_stored = [sem(f"rel_stored{k}") for k in range(GROUP)]
        rel_freed = sem("rel_freed")
        self_done = sem("self_done")
        self_added = sem("self_added")
        out_stored = sem("out_stored")
        carried = sem("carried")

        block = ctx.enter_context(nc.Block())

        def pipeline(eng, rnd, ahead, cycle, end=None, ranges=True):
            def at(step, i, k, win):
                step(rnd * NCH + 2 * i + k, rnd * PAIRS + i + k // 2, k % 2, 2 * i + k, win)

            def whole(i, k, first=False, last=False):
                c, before, after = 2 * i + k, 0 if first else 1, 0 if last else 1
                w = windows(eng, c - before, 1 + before + after) if ranges else []
                pairs = [tuple(w[2 * x:2 * x + 2]) for x in range(len(w) // 2)]
                if not last:
                    at(ahead, i, k + 1, {x - before - 1: v for x, v in enumerate(pairs)})
                at(cycle, i, k, {x - before: v for x, v in enumerate(pairs)})
                if last and end is not None:
                    at(end, i, k, {x - before: v for x, v in enumerate(pairs)})

            at(ahead, 0, 0, {0: tuple(windows(eng, 0, 1))} if ranges else {})
            whole(0, 0, first=True)
            with eng.Fori(0, PAIRS - 1) as i:
                whole(i, 1)
                whole(i, 2)
            whole(PAIRS - 1, 1, last=True)

        def steps(eng, first, each, tail=None):
            first()
            with eng.Fori(0, NG - 1) as j:
                each(j, True)
            each(NG - 1, False)

        def carry_wait(eng):
            eng.sem_inc(carried, 1)

        def windows(eng, c, count):
            return nc.values_load_multi_w_load_instructions(
                range_row[0:1, ds(2 * c, 2 * count)], engines=(eng.engine,), min_val=0, max_val=NW - 1,
                skip_runtime_bounds_check_because="the destinations are nodes")[1]

        @block.sync
        def _(sp):
            sp.sem_inc(rel_freed, GROUP)
            sp.dma_start(chunk_dst[:, :, :], dst_rows.rearrange("(p a) e -> p a e", a=2)).then_inc(loaded, 16)
            sp.dma_start(dst_sb[:, :], dst).then_inc(loaded, 16)
            sp.dma_start(xaT[0:D, :], xT).then_inc(loaded, 16)
            sp.dma_start(src_sb[:, :], src).then_inc(loaded, 16)
            for l in range(LAYERS):
                sp.dma_start(w_ij_all[:, l, 0:D], msg_w[l, 0:D, :]).then_inc(loaded, 16)
                sp.dma_start(w_ij_all[:, l, D:], msg_w[l, D:2 * D, :]).then_inc(loaded, 16)
            for l in range(LAYERS):
                sp.dma_start(b_msg[:, l, :, :], msg_b[l:l + 1, :].unsqueeze(1).to_broadcast([1, GROUP, D])
                             ).then_inc(loaded, 16)
            sp.wait_ge(const_pool, 1)
            for u in range(TILES):
                sp.dma_start(w_e_diag[u * NE:(u + 1) * NE, :, u * D:(u + 1) * D],
                             msg_w[:, 2 * D:2 * D + NE, :].rearrange("l i o -> i l o")).then_inc(diag_loaded, 16)
            late = [(w_upd_all[:, :, :], upd_w.rearrange("l i o -> i l o")),
                    (rel_sb[:, :], etype),
                    (xres[:, :, :], x_rows.rearrange("(w p) d -> p w d", p=P))]
            late += [(b_upd_all[:, l:l + 1], upd_b[l, :].unsqueeze(1)) for l in range(LAYERS)]
            for r, (ba, co, ws, bi) in enumerate([(bases1, coef1, wself1, bias1),
                                                  (bases2, coef2, wself2, bias2)]):
                late += [(bases[:, r, :, :], ba.rearrange("b i o -> i b o")),
                         (coef[:, r, :, :], co.unsqueeze(0).to_broadcast([D, NR, NB])),
                         (w_rel[:, r, NR * D:], ws),
                         (bias_bc[:, r, :], bi.unsqueeze(0).to_broadcast([P, D]))]
            assert len(late) == LATE
            for to, of in late:
                sp.dma_start(to, of).then_inc(late_loaded, 16)
            sp.wait_ge(range_made, 4)
            sp.dma_start(range_dram.rearrange("(p a) b -> p (a b)", a=2),
                         window_range[:, :, :].rearrange("p a b -> p (a b)")).then_inc(range_stored, 16)
            sp.dma_start(base_dram.rearrange("(p a) -> p a", a=2), window_base[:, :]).then_inc(range_stored, 16)
            sp.wait_ge(range_stored, 32)
            sp.dma_start(range_row[:, :], range_dram.rearrange("(o c) b -> o (c b)", o=1)).then_inc(range_loaded, 16)
            sp.dma_start(base_bc[:, :], base_dram.unsqueeze(0).to_broadcast([P, NCH])).then_inc(range_loaded, 16)


            def load_indices(S, c, q, rows):
                sp.dma_start(idx[q][:, :], rows[:, ds(c * TILES, TILES)]).then_inc(S["idx_loaded"][q], 16)

            def load_attributes(c, n, q):
                sp.wait_ge(M["pre_done"], n + 1)
                sp.dma_start(attr[q][:, :], edge_attr[ds(c, 1), :, :].rearrange("a f e -> (a f) e")
                             ).then_inc(M["attr_loaded"][q], 16)

            def msg_tables(l):
                with sp.Fori(0, NG) as j:
                    sp.wait_ge(b_copied, l * NG + j + 2)
                    sp.dma_start(msg_table[ds(j * GN, GN), :].rearrange("(w p) d -> p w d", p=P),
                                 b_rows[:, ds(j * GROUP, GROUP), :]).then_inc(msg_stored, 16)

            def msg_chunks(l):
                with sp.Fori(1, PAIRS) as i:
                    for q in range(2):
                        sp.wait_ge(M["gathered"][q], 16 * TILES * (l * PAIRS + i))
                        load_indices(M, 2 * i + q, q, src_sb)
                        load_attributes(2 * i + q, l * NCH + 2 * i + q, q)

            for q in range(2):
                load_indices(M, q, q, src_sb)
                load_attributes(q, q, q)
            msg_tables(0)
            with sp.Fori(0, LAYERS - 1) as l:
                msg_chunks(l)
                for q in range(2):
                    sp.wait_ge(M["gathered"][q], 16 * TILES * (l + 1) * PAIRS)
                    load_indices(M, q, q, src_sb)
                    load_attributes(q, (l + 1) * NCH + q, q)
                msg_tables(l + 1)
            msg_chunks(LAYERS - 1)

            sp.wait_ge(setup_dve, 3)
            for q in range(2):
                sp.wait_ge(M["gathered"][q], 16 * TILES * LAYERS * PAIRS)
                load_indices(R, q, q, rel_sb)
            with sp.Fori(0, RLAYERS) as r:
                with sp.Fori(0, NG) as j:
                    t = r * NG + j
                    for k in range(GROUP + LAG):
                        if k < GROUP:
                            sp.wait_ge(rel_copied, t * GROUP + k + 4)
                            sp.dma_start(rel_table[ds((j * GROUP + k) * (P * NR), P * NR), :]
                                         .rearrange("(p a) d -> p (a d)", a=NR),
                                         rel_rows[k]).then_inc(rel_stored[k], 16)
                        if k >= LAG:
                            sp.wait_ge(rel_stored[k - LAG], (t + 1) * 16)
                            sp.sem_inc(rel_freed, 1)
                with sp.Fori(1, PAIRS) as i:
                    for q in range(2):
                        sp.wait_ge(R["gathered"][q], 16 * TILES * (r * PAIRS + i))
                        load_indices(R, 2 * i + q, q, rel_sb)
                with sp.If(r < RLAYERS - 1):
                    for q in range(2):
                        sp.wait_ge(R["gathered"][q], 16 * TILES * (r + 1) * PAIRS)
                        load_indices(R, q, q, rel_sb)

            whole = N // P
            sp.wait_ge(norm, 2 * LN_STEPS - 1)
            sp.dma_start(out[0:whole * P, :].rearrange("(w p) d -> p w d", p=P),
                         xres[:, 0:whole, :]).then_inc(out_stored, 16)
            if N % P:
                sp.dma_start(out[whole * P:N, :], xres[0:N % P, whole, :]).then_inc(out_stored, 16)
            sp.wait_ge(out_stored, 16 * (1 + bool(N % P)))

        @block.gpsimd
        def _(pool):
            pool.memset(w_e_diag[:, :, :], 0.0).then_inc(const_pool, 1)
            pool.iota(col_id[:, :], [[1, P]], base=0, channel_multiplier=0).then_inc(const_pool, 1)
            pool.memset(ones[:, :], 1.0).then_inc(const_pool, 1)
            pool.memset(ident_f[:, :], 0.0).then_inc(const_pool, 1)
            pool.memset(eps_col[:, :], EPS).then_inc(const_pool, 1)
            pool.wait_ge(const_pool, 5)
            pool.affine_select(ident_f[:, :], ident_f[:, :], [[-1, P]], ALU.not_equal, 1.0, base=0,
                               channel_multiplier=1).then_inc(const_pool, 1)
            pool.iota(node_id[:, :], [[1, NP]], base=0, channel_multiplier=0).then_inc(const_pool, 1)

            def gather(S, table, m, n, q, used):
                pool.wait_ge(S["idx_loaded"][q], 16 * (m + 1))
                pool.wait_ge(S[used], n + 1)
                carry_wait(pool)
                for u in range(TILES):
                    pool.indirect_dma_start(gath[q][:, u, :], None, table,
                                            bass.IndirectOffsetOnAxis(ap=idx[q][:, u:u + 1], axis=0)
                                            ).then_inc(S["gathered"][q], 16)

            with pool.Fori(0, LAYERS) as l:
                pool.wait_ge(msg_stored, 16 * NG * (l + 1))
                carry_wait(pool)
                with pool.Fori(0, PAIRS) as i:
                    for q in range(2):
                        gather(M, msg_table, l * PAIRS + i, l * NCH + 2 * i + q, q, "z_done")
            with pool.Fori(0, RLAYERS) as r:
                for k in range(GROUP):
                    pool.wait_ge(rel_stored[k], 16 * NG * (r + 1))
                carry_wait(pool)
                with pool.Fori(0, PAIRS) as i:
                    for q in range(2):
                        gather(R, rel_table, r * PAIRS + i, r * NCH + 2 * i + q, q, "rest_done")

        @block.scalar
        def _(act):
            visits = act.alloc_register("act_visits")
            act.reg_mov(visits, 0)
            act.sem_inc(M["hotT_copied"], 1)
            act.sem_inc(b_copied, 1)
            act.sem_inc(aggT_copied, 2)
            act.sem_inc(x_updated, 2)
            act.sem_inc(hT_copied, 2)
            act.sem_inc(rel_copied, 3)

            def msg_ahead(n, m, q, c, win):
                w0, w1 = win[0]
                act.wait_ge(M["hotT_done"], n + 1)
                act.activation(hotT[:, :, :], hotT_ps[:, :, :], ACT.Copy).then_inc(M["hotT_copied"], 1)
                with act.If(w0 < w1):
                    with act.Fori(w0, w1):
                        k = act.snap(visits, min_val=0)
                        act.wait_ge(M["xa_T"], k + 2)
                        act.activation(x_hotT[:, :, :], x_hotT_ps[:, :, :], ACT.Copy).then_inc(M["xa_copied"], 1)
                        act.reg_add(visits, visits, 1)

            def msg_cycle(n, m, q, c, win):
                z = pre[q][:, :].rearrange("p (u d) -> p u d", d=D)
                act.wait_ge(M["z_done"], n + 3)
                act.wait_ge(M["sums_done"], n + 1)
                act.activation(m3[q][:, :, 0:D], z, ACT.Relu).then_inc(M["hi_done"], 1)
                act.wait_ge(M["rest_done"], n + 1)
                act.activation(m3[q][:, :, D:2 * D], z, ACT.Copy).then_inc(M["mid_done"], 1)

            def set_weights(l):
                act.wait_ge(x_updated, l * 2 * NG + 2)
                act.wait_ge(ab_done, l * NG + 2)
                for to, of in [(w_upd[:, :], w_upd_all[:, ds(l, 1), :]),
                               (b_upd[:, :], b_upd_all[:, ds(l, 1)])]:
                    if len(of.shape) == 3:
                        of = of.rearrange("p a d -> p (a d)")
                    act.activation(to, of, ACT.Copy).then_inc(weights_set, 1)

            def set_table_weights(l):
                act.activation(w_ij[:, :], w_ij_all[:, ds(l, 1), :].rearrange("p a d -> p (a d)"),
                               ACT.Copy).then_inc(weights_set, 1)

            def msg_tables(t, j):
                act.wait_ge(b_done, t + 1)
                act.activation(b_rows[:, ds(j * GROUP, GROUP), :],
                               x_sums[:, 0:GROUP * D].rearrange("p (w d) -> p w d", d=D),
                               ACT.Copy).then_inc(b_copied, 1)
                act.wait_ge(ab_done, t + 2)
                act.activation(a3[:, ds(j * GROUP, GROUP), 0:D],
                               a_ps[:, 0:GROUP * D].rearrange("p (w d) -> p w d", d=D),
                               ACT.Copy).then_inc(a_hi, 1)
                act.wait_ge(a_rested, t + 1)
                act.activation(a3[:, ds(j * GROUP, GROUP), D:2 * D], a_rest[:, :, :], ACT.Copy).then_inc(a_mid, 1)

            def copy_aggT(l, j):
                for s, (a, b) in enumerate(HALF):
                    act.wait_ge(aggT_done, 2 * (l * NG + j) + s + 3)
                    act.activation(xaT[D:2 * D, ds(j * GN + a * P, (b - a) * P)],
                                   pre[s][0:D, 0:(b - a) * P], ACT.Copy).then_inc(aggT_copied, 1)

            def update(l, j):
                act.wait_ge(x_kept, l * NG + j + 1)
                for s, (a, b) in enumerate(HALF):
                    act.wait_ge(upd_done, 2 * (l * NG + j) + s + 1)
                    act.activation(stage_T[:, a * P:b * P], sums[s][0:D, 0:(b - a) * P],
                                   ACT.Relu, bias=b_upd[:, :]).then_inc(x_updated, 1)

            act.wait_ge(loaded, LOADED)
            with act.Fori(0, NG) as j:
                act.wait_ge(ab_done, j + 1)
                act.activation(stage_T[:, :], xaT[0:D, ds(j * GN, GN)], ACT.Copy).then_inc(xT_staged, 1)
                msg_tables(j, j)
            act.wait_ge(late_loaded, 16 * LATE)
            act.wait_ge(range_loaded, 32)
            with act.Fori(0, LAYERS - 1) as l:
                set_weights(l)
                set_table_weights(l + 1)
                pipeline(act, l, msg_ahead, msg_cycle)

                def each(j, more):
                    act.wait_ge(ab_done, (l + 1) * NG + j + 1)
                    update(l, j)
                    if more:
                        copy_aggT(l, j + 1)
                    msg_tables((l + 1) * NG + j, j)

                steps(act, lambda: copy_aggT(l, 0), each)
            set_weights(LAYERS - 1)
            pipeline(act, LAYERS - 1, msg_ahead, msg_cycle)

            def each(j, more):
                act.wait_ge(x3_rows, j + 1)
                update(LAYERS - 1, j)
                if more:
                    copy_aggT(LAYERS - 1, j + 1)

            steps(act, lambda: copy_aggT(LAYERS - 1, 0), each)
            act.wait_ge(var_done, 1)
            act.activation(rstd[:, :], var[:, :], ACT.Sqrt, bias=eps_col[:, :]).then_inc(std_done, 1)

            def rel_ahead(n, m, q, c, win):
                pass

            def rel_cycle(n, m, q, c, win):
                act.wait_ge(R["gathered"][q], 16 * TILES * (m + 1))
                act.wait_ge(R["sums_done"], n + 1)
                act.activation(m3[q][:, :, 0:D], gath[q][:, :, :], ACT.Copy).then_inc(R["hi_done"], 1)
                act.wait_ge(R["rest_done"], n + 3)
                act.activation(m3[q][:, :, D:2 * D], pre[q][:, :].rearrange("p (u d) -> p u d", d=D),
                               ACT.Copy).then_inc(R["mid_done"], 1)

            def copy_hT(r, j, s):
                a, b = HALF[s]
                act.wait_ge(hT_done, 2 * (r * NG + j) + s + 3)
                act.activation(stage_T[:, a * P:b * P], rows_T[s][0:D, 0:(b - a) * P],
                               ACT.Copy).then_inc(hT_copied, 1)

            with act.Fori(0, RLAYERS) as r:
                def each(j, more):
                    for s, (a, b) in enumerate(HALF):
                        for k in range(a, b):
                            t = (r * NG + j) * GROUP + k
                            act.wait_ge(rel_done, t + 1)
                            act.wait_ge(rel_freed, t + 1)
                            act.activation(rel_rows[k], rel_ps[k % 3][:, :], ACT.Copy).then_inc(rel_copied, 1)
                        if more:
                            copy_hT(r, j + 1, s)

                steps(act, lambda: [copy_hT(r, 0, s) for s in range(2)], each)
                pipeline(act, r, rel_ahead, rel_cycle, ranges=False)
            act.wait_ge(var_done, 2)
            act.activation(rstd[:, :], var[:, :], ACT.Sqrt, bias=eps_col[:, :]).then_inc(std_done, 1)

        @block.tensor
        def _(pe):
            visits_a = pe.alloc_register("pe_visits_a")
            visits_b = pe.alloc_register("pe_visits_b")
            visits_r = pe.alloc_register("pe_visits_r")
            for reg in (visits_a, visits_b, visits_r):
                pe.reg_mov(reg, 0)
            pe.sem_inc(M["sums_done"], 2)
            pe.sem_inc(R["sums_done"], 2)
            pe.sem_inc(M["pre_done"], 2)
            pe.sem_inc(M["xa_T"], 1)
            pe.sem_inc(ab_done, 1)
            pe.sem_inc(aggT_done, 2)
            pe.sem_inc(x3_rows, 1)
            pe.sem_inc(hT_done, 2)

            def transposes(to, of):
                for u in range(TILES):
                    last = nc.tensor.transpose(to[:, u, :], of[:, u, :], ident_b[:, :])
                return last

            def expand(to, of, w, stop):
                for u in range(TILES):
                    for k in range(3):
                        last = nc.tensor.matmul(to[:, u * D:(u + 1) * D], of[:, u, :],
                                                a3[:, ds(w, 1), k * D:(k + 1) * D].rearrange("p a d -> p (a d)"),
                                                start=False, stop=stop and k == 2 and u == TILES - 1)
                return last

            def sum_up(to, hots, parts):
                for u in range(TILES):
                    last = nc.tensor.matmul(to[:, 0:3 * D], hots[:, u, :], parts[:, u, :],
                                            start=u == 0, stop=u == TILES - 1)
                return last

            def msg_ahead(l, n, m, q, c, win):
                w0, w1 = win[0]
                pe.wait_ge(M["attr_loaded"][q], 16 * (m + 1))
                pe.wait_ge(M["lo_done"], n + 1)
                nc.tensor.matmul(pre[q][:, :], attr[q][:, :],
                                 w_e_diag[:, ds(l, 1), :].rearrange("p a d -> p (a d)"), start=True, stop=False)
                pe.wait_ge(M["hot_built"], n + 1)
                pe.wait_ge(M["hotT_copied"], n + 1)
                transposes(hotT_ps, hot[q]).then_inc(M["hotT_done"], 1)
                with pe.If(w0 < w1):
                    with pe.Fori(w0, w1) as w:
                        k = pe.snap(visits_a, min_val=0)
                        pe.wait_ge(M["xa_built"], k + 1)
                        transposes(x_hotT_ps, x_hotA).then_inc(M["xa_T"], 1)
                        pe.wait_ge(M["xa_copied"], k + 1)
                        expand(pre[q], x_hotT, w + 1, False)
                        pe.reg_add(visits_a, visits_a, 1)
                pe.wait_ge(M["hotT_copied"], n + 2)
                expand(pre[q], hotT, w0, True).then_inc(M["pre_done"], 1)

            def sums_cycle(S, visits):
                def run(n, m, q, c, win):
                    w0, w1 = win[0]
                    with pe.If(w0 < w1):
                        with pe.Fori(w0, w1):
                            k = pe.snap(visits, min_val=0)
                            pe.wait_ge(S["xb_built"], k + 1)
                            sum_up(x_sums, x_hotB, m3[q]).then_inc(S["xb_sums"], 1)
                            pe.reg_add(visits, visits, 1)
                    pe.wait_ge(S["agg_added"], n + 1)
                    pe.wait_ge(S["lo_done"], n + 3)
                    sum_up(sums[q], hot[q], m3[q]).then_inc(S["sums_done"], 1)
                return run

            def rel_ahead(n, m, q, c, win):
                pe.wait_ge(R["hot_built"], n + 1)
                carry_wait(pe)

            def msg_tables(t, weights, bias):
                pe.wait_ge(b_copied, t + 1)
                for w in range(GROUP):
                    last = nc.tensor.matmul(x_sums[:, w * D:(w + 1) * D], stage_T[:, w * P:(w + 1) * P],
                                            weights[:, D:2 * D], start=True, stop=True)
                last.then_inc(b_done, 1)
                pe.wait_ge(a_lo, t + 1)
                nc.tensor.matmul(a_ps[:, 0:GROUP * D], ones[:, :], bias, start=True, stop=False)
                for w in range(GROUP):
                    last = nc.tensor.matmul(a_ps[:, w * D:(w + 1) * D], stage_T[:, w * P:(w + 1) * P],
                                            weights[:, 0:D], start=False, stop=w == GROUP - 1)
                last.then_inc(ab_done, 1)

            def transpose_agg(l, j):
                for s, (a, b) in enumerate(HALF):
                    h = 2 * (l * NG + j) + s
                    pe.wait_ge(agg_staged, h + 1)
                    pe.wait_ge(aggT_copied, h + 1)
                    carry_wait(pe)
                    for w in range(a, b):
                        last = nc.tensor.transpose(pre[s][0:D, (w - a) * P:(w - a + 1) * P],
                                                   stage_rows[:, w, :], ident_f[:, :])
                    last.then_inc(aggT_done, 1)

            def update(l, j):
                for s, (a, b) in enumerate(HALF):
                    h = 2 * (l * NG + j) + s
                    pe.wait_ge(aggT_copied, h + 3)
                    pe.wait_ge(x_updated, h + 1)
                    nc.tensor.matmul(sums[s][0:D, 0:(b - a) * P], w_upd[:, :],
                                     xaT[:, ds(j * GN + a * P, (b - a) * P)],
                                     start=True, stop=True).then_inc(upd_done, 1)

            def chunks_end(S, rnd):
                pe.wait_ge(S["agg_added"], (rnd + 1) * NCH + 2)

            pe.wait_ge(setup_dve, 1)
            pe.wait_ge(const_pool, 7)
            with pe.Fori(0, NG) as j:
                pe.wait_ge(xT_staged, j + 1)
                msg_tables(j, w_ij_all[:, 0, :], b_msg[:, 0, :, :].rearrange("p w d -> p (w d)"))
            with pe.Fori(0, LAYERS - 1) as l:
                pe.wait_ge(a_lo, (l + 1) * NG + 1)
                pe.wait_ge(weights_set, 3 * (l + 1))
                carry_wait(pe)
                pe.wait_ge(range_loaded, 32)
                pe.wait_ge(diag_loaded, 16 * TILES)
                pipeline(pe, l, lambda *at: msg_ahead(l, *at), sums_cycle(M, visits_b))
                chunks_end(M, l)
                carry_wait(pe)

                def each(j, more):
                    update(l, j)
                    if more:
                        transpose_agg(l, j + 1)
                    pe.wait_ge(x_updated, 2 * (l * NG + j) + 4)
                    msg_tables((l + 1) * NG + j, w_ij,
                               b_msg[:, ds(l + 1, 1), :, :].rearrange("p a w d -> p (a w d)"))

                steps(pe, lambda: transpose_agg(l, 0), each)
            pe.wait_ge(a_lo, LAYERS * NG + 1)
            pe.wait_ge(weights_set, 3 * LAYERS - 1)
            pipeline(pe, LAYERS - 1, lambda *at: msg_ahead(LAYERS - 1, *at), sums_cycle(M, visits_b))
            chunks_end(M, LAYERS - 1)

            def each(j, more):
                update(LAYERS - 1, j)
                if more:
                    transpose_agg(LAYERS - 1, j + 1)
                pe.wait_ge(x_updated, 2 * ((LAYERS - 1) * NG + j) + 4)
                pe.wait_ge(x3_added, j + 1)
                carry_wait(pe)
                for w in range(GROUP):
                    last = nc.tensor.transpose(x_sums[:, w * D:(w + 1) * D], stage_T[:, w * P:(w + 1) * P],
                                               ident_f[0:D, 0:D])
                last.then_inc(x3_rows, 1)

            steps(pe, lambda: transpose_agg(LAYERS - 1, 0), each)
            pe.wait_ge(x3_added, NG + 1)

            def transpose_h(r, j, s):
                a, b = HALF[s]
                h = 2 * (r * NG + j) + s
                pe.wait_ge(h_staged, h + 1)
                pe.wait_ge(hT_copied, h + 1)
                carry_wait(pe)
                for w in range(a, b):
                    last = nc.tensor.transpose(rows_T[s][0:D, (w - a) * P:(w - a + 1) * P],
                                               stage_rows[:, w, :], ident_f[:, :])
                last.then_inc(hT_done, 1)

            with pe.Fori(0, RLAYERS) as r:
                def each(j, more):
                    for s, (a, b) in enumerate(HALF):
                        h = 2 * (r * NG + j) + s
                        pe.wait_ge(self_added, h + 1)
                        for k in range(a, b):
                            pe.wait_ge(hT_copied, h + 3)
                            back = k if k >= 3 else (GROUP - 1 - (GROUP - 1 - k) % 3) - GROUP + 3
                            pe.wait_ge(rel_copied, (r * NG + j) * GROUP + back + 1)
                            carry_wait(pe)
                            lhsT = stage_T[:, k * P:(k + 1) * P]
                            nc.tensor.matmul(rel_ps[k % 3][:, :], lhsT,
                                             w_rel[:, ds(r, 1), 0:NR * D].rearrange("p a d -> p (a d)"),
                                             start=True, stop=True).then_inc(rel_done, 1)
                            last = nc.tensor.matmul(sums[s][:, (k - a) * D:(k - a + 1) * D], lhsT,
                                                    w_rel[:, ds(r, 1), NR * D:].rearrange("p a d -> p (a d)"),
                                                    start=True, stop=True)
                        last.then_inc(self_done, 1)
                        if more:
                            transpose_h(r, j + 1, s)

                steps(pe, lambda: [transpose_h(r, 0, s) for s in range(2)], each)
                pe.wait_ge(self_added, 2 * (r + 1) * NG + 2)
                pe.wait_ge(rel_copied, (r + 1) * NG * GROUP + 3)
                carry_wait(pe)
                pipeline(pe, r, rel_ahead, sums_cycle(R, visits_r))
                chunks_end(R, r)
                carry_wait(pe)

        @block.vector
        def _(dve):
            visits_a = dve.alloc_register("dve_visits_a")
            visits_b = dve.alloc_register("dve_visits_b")
            visits_r = dve.alloc_register("dve_visits_r")
            for reg in (visits_a, visits_b, visits_r):
                dve.reg_mov(reg, 0)
            for S in (M, R):
                dve.sem_inc(S["lo_done"], 2)
                dve.sem_inc(S["agg_added"], 2)
                dve.sem_inc(S["xb_added"], 1)
            dve.sem_inc(M["z_done"], 2)
            dve.sem_inc(R["rest_done"], 2)
            dve.sem_inc(a_lo, 1)
            dve.sem_inc(x_kept, 1)
            dve.sem_inc(x3_added, 1)
            dve.sem_inc(self_added, 2)

            dve.wait_ge(const_pool, 7)
            nc.vector.tensor_copy(col_ps[:, :], col_id[:, :])
            nc.vector.tensor_copy(ident_b[:, :], ident_f[:, :]).then_inc(setup_dve, 1)
            dve.wait_ge(loaded, LOADED)
            nc.vector.tensor_reduce(extreme[:, :, 0], chunk_dst[:, :, :], AX.X, ALU.min).then_inc(range_made, 1)
            nc.vector.tensor_reduce(extreme[:, :, 1], chunk_dst[:, :, :], AX.X, ALU.max).then_inc(range_made, 1)
            dve.wait_ge(range_made, 2)
            nc.vector.tensor_scalar(window_range[:, :, :], extreme[:, :, :], 7, None,
                                    ALU.arith_shift_right).then_inc(range_made, 1)
            dve.wait_ge(range_made, 3)
            nc.vector.tensor_scalar(window_base[:, :], window_range[:, :, 0], float(P), None,
                                    ALU.mult).then_inc(range_made, 1)
            cols = col_ps[:, :].unsqueeze(1).to_broadcast([P, TILES, P])

            def build_first(S, c, n, q):
                dve.wait_ge(S["sums_done"], n + 1)
                nc.vector.tensor_tensor(hot[q][:, :, :], cols,
                                        dst_rel[:, ds(c * TILES, TILES)].unsqueeze(2).to_broadcast([P, TILES, P]),
                                        ALU.is_equal).then_inc(S["hot_built"], 1)

            def build(to, c, w):
                return nc.vector.tensor_tensor(
                    to, node_id[:, ds(w * P, P)].unsqueeze(1).to_broadcast([P, TILES, P]),
                    dst_sb[:, ds(c * TILES, TILES)].unsqueeze(2).to_broadcast([P, TILES, P]), ALU.is_equal)

            def add_extra(S, visits, c, n, q, w0, w1):
                with dve.If(w0 < w1):
                    with dve.Fori(w0, w1) as w:
                        k = dve.snap(visits, min_val=0)
                        dve.wait_ge(S["xb_added"], k + 1)
                        dve.wait_ge(S["agg_added"], n + 2)
                        build(x_hotB[:, :, :], c, w + 1).then_inc(S["xb_built"], 1)
                        dve.wait_ge(S["xb_sums"], k + 1)
                        nc.vector.tensor_reduce(x_part[:, :], x_sums[:, 0:3 * D].rearrange("p (k d) -> p d k", d=D),
                                                AX.X, ALU.add).then_inc(S["xb_part"], 1)
                        dve.wait_ge(S["xb_part"], k + 1)
                        to = agg[:, ds(w + 1, 1), :].rearrange("p a d -> p (a d)")
                        nc.vector.tensor_tensor(to, to, x_part[:, :], ALU.add).then_inc(S["xb_added"], 1)
                        dve.reg_add(visits, visits, 1)

            def add_first(S, visits, n, q, w0):
                k = dve.snap(visits, min_val=0)
                dve.wait_ge(S["xb_added"], k + 1)
                dve.wait_ge(S["agg_added"], n + 2)
                dve.wait_ge(S["sums_done"], n + 3)
                nc.vector.tensor_reduce(part[:, :], sums[q][:, 0:3 * D].rearrange("p (k d) -> p d k", d=D),
                                        AX.X, ALU.add).then_inc(S["part_done"], 1)
                dve.wait_ge(S["part_done"], n + 1)
                to = agg[:, ds(w0, 1), :].rearrange("p a d -> p (a d)")
                nc.vector.tensor_tensor(to, to, part[:, :], ALU.add).then_inc(S["agg_added"], 1)

            def msg_ahead(n, m, q, c, win):
                w0, w1 = win[0]
                build_first(M, c, n, q)
                with dve.If(w0 < w1):
                    with dve.Fori(w0, w1) as w:
                        k = dve.snap(visits_a, min_val=0)
                        dve.wait_ge(M["xa_T"], k + 1)
                        build(x_hotA[:, :, :], c, w + 1).then_inc(M["xa_built"], 1)
                        dve.reg_add(visits_a, visits_a, 1)

            def msg_cycle(n, m, q, c, win):
                z = pre[q][:, :].rearrange("p (u d) -> p u d", d=D)
                w0, w1 = win[0]
                dve.wait_ge(M["pre_done"], n + 3)
                dve.wait_ge(M["gathered"][q], 16 * TILES * (m + 1))
                nc.vector.tensor_tensor(z, z, gath[q][:, :, :], ALU.add).then_inc(M["z_done"], 1)
                if -1 in win:
                    add_first(M, visits_b, n - 1, 1 - q, win[-1][0])
                dve.wait_ge(M["hi_done"], n + 1)
                nc.vector.scalar_tensor_tensor(z, z, 0.0, m3[q][:, :, 0:D], ALU.max,
                                               ALU.subtract).then_inc(M["rest_done"], 1)
                dve.wait_ge(M["mid_done"], n + 1)
                nc.vector.tensor_tensor(m3[q][:, :, 2 * D:], z, m3[q][:, :, D:2 * D],
                                        ALU.subtract).then_inc(M["lo_done"], 1)
                add_extra(M, visits_b, c, n, q, w0, w1)

            def split_tables(t, j):
                rows = a_ps[:, 0:GROUP * D].rearrange("p (w d) -> p w d", d=D)
                to = a3[:, ds(j * GROUP, GROUP), :]
                dve.wait_ge(a_hi, t + 1)
                nc.vector.tensor_tensor(a_rest[:, :, :], rows, to[:, :, 0:D], ALU.subtract).then_inc(a_rested, 1)
                dve.wait_ge(a_mid, t + 1)
                nc.vector.tensor_tensor(to[:, :, 2 * D:], a_rest[:, :, :], to[:, :, D:2 * D],
                                        ALU.subtract).then_inc(a_lo, 1)

            def stage_agg(l, j):
                for s, (a, b) in enumerate(HALF):
                    h = 2 * (l * NG + j) + s
                    dve.wait_ge(aggT_done, h + 1)
                    nc.vector.tensor_copy(stage_rows[:, a:b, :], agg[:, ds(j * GROUP + a, b - a), :]
                                          ).then_inc(agg_staged, 1)

            def keep_x(l, j):
                dve.wait_ge(x_updated, 2 * (l * NG + j) + 4)
                nc.vector.tensor_copy(xaT[0:D, ds(j * GN, GN)], stage_T[:, :]).then_inc(x_kept, 1)

            def msg_end(n, m, q, c, win):
                add_first(M, visits_b, n, q, win[0][0])

            nc.vector.memset(agg[:, :, :], 0.0).then_inc(agg_zeroed, 1)
            with dve.Fori(0, NG) as j:
                split_tables(j, j)
            dve.wait_ge(range_loaded, 32)
            nc.vector.tensor_tensor(dst_rel[:, :].rearrange("p (c u) -> p c u", u=TILES),
                                    dst_sb[:, :].rearrange("p (c u) -> p c u", u=TILES),
                                    base_bc[:, :].unsqueeze(2).to_broadcast([P, NCH, TILES]),
                                    ALU.subtract).then_inc(setup_dve, 1)
            dve.wait_ge(setup_dve, 2)

            dve.wait_ge(late_loaded, 16 * LATE)
            chain = 0
            for r in range(RLAYERS):
                w = w_rel[:, r, 0:NR * D].rearrange("p (r d) -> p r d", d=D)
                for b in range(NB):
                    to = w if b == 0 else w_tmp[:, :, :]
                    nc.vector.tensor_tensor(to, bases[:, r, b, :].unsqueeze(1).to_broadcast([D, NR, D]),
                                            coef[:, r, :, b].unsqueeze(2).to_broadcast([D, NR, D]),
                                            ALU.mult).then_inc(rel_weights, 1)
                    chain += 1
                    dve.wait_ge(rel_weights, chain)
                    if b:
                        nc.vector.tensor_tensor(w, w, w_tmp[:, :, :], ALU.add).then_inc(rel_weights, 1)
                        chain += 1
                        dve.wait_ge(rel_weights, chain)
            nc.vector.scalar_tensor_tensor(rel_sb[:, :], src_sb[:, :], float(NR), rel_sb[:, :],
                                           ALU.mult, ALU.add).then_inc(setup_dve, 1)
            with dve.Fori(0, LAYERS - 1) as l:
                dve.wait_ge(agg_zeroed, l + 1)
                carry_wait(dve)
                pipeline(dve, l, msg_ahead, msg_cycle, msg_end)
                dve.wait_ge(M["agg_added"], (l + 1) * NCH + 2)
                carry_wait(dve)

                def each(j, more):
                    if more:
                        stage_agg(l, j + 1)
                    keep_x(l, j)
                    split_tables((l + 1) * NG + j, j)

                steps(dve, lambda: stage_agg(l, 0), each)
                nc.vector.memset(agg[:, :, :], 0.0).then_inc(agg_zeroed, 1)
            dve.wait_ge(agg_zeroed, LAYERS)
            pipeline(dve, LAYERS - 1, msg_ahead, msg_cycle, msg_end)
            dve.wait_ge(M["agg_added"], LAYERS * NCH + 2)

            def each(j, more):
                if more:
                    stage_agg(LAYERS - 1, j + 1)
                keep_x(LAYERS - 1, j)
                dve.wait_ge(x3_rows, j + 2)
                to = xres[:, ds(j * GROUP, GROUP), :]
                nc.vector.tensor_tensor(to, to, x_sums[:, 0:GROUP * D].rearrange("p (w d) -> p w d", d=D),
                                        ALU.add).then_inc(x3_added, 1)

            steps(dve, lambda: stage_agg(LAYERS - 1, 0), each)
            dve.wait_ge(x3_added, NG + 1)

            def layer_norm(k, copy_to):
                at = k * LN_STEPS
                bc = [P, NW, D]

                def step(ins):
                    nonlocal at
                    at += 1
                    ins.then_inc(norm, 1)
                    dve.wait_ge(norm, at)

                step(nc.vector.tensor_reduce(mean[:, :], xres[:, :, :], AX.X, ALU.add))
                step(nc.vector.tensor_scalar(mean[:, :], mean[:, :], 1.0 / D, None, ALU.mult))
                step(nc.vector.tensor_tensor(xres[:, :, :], xres[:, :, :],
                                             mean[:, :].unsqueeze(2).to_broadcast(bc), ALU.subtract))
                step(nc.vector.tensor_tensor(b_rows[:, :, :], xres[:, :, :], xres[:, :, :], ALU.mult))
                step(nc.vector.tensor_reduce(var[:, :], b_rows[:, :, :], AX.X, ALU.add))
                nc.vector.tensor_scalar(var[:, :], var[:, :], 1.0 / D, None, ALU.mult).then_inc(var_done, 1)
                dve.wait_ge(std_done, k + 1)
                step(nc.vector.reciprocal(rstd[:, :], rstd[:, :]))
                step(nc.vector.tensor_tensor(newton[:, :], rstd[:, :], rstd[:, :], ALU.mult))
                step(nc.vector.tensor_scalar(var[:, :], var[:, :], EPS, None, ALU.add))
                step(nc.vector.tensor_tensor(newton[:, :], newton[:, :], var[:, :], ALU.mult))
                step(nc.vector.tensor_scalar(newton[:, :], newton[:, :], -0.5, 1.5, ALU.mult, ALU.add))
                step(nc.vector.tensor_tensor(rstd[:, :], rstd[:, :], newton[:, :], ALU.mult))
                step(nc.vector.tensor_tensor(xres[:, :, :], xres[:, :, :],
                                             rstd[:, :].unsqueeze(2).to_broadcast(bc), ALU.mult))
                if copy_to is not None:
                    step(nc.vector.tensor_copy(copy_to, xres[:, :, :]))

            layer_norm(0, agg[:, :, :])

            def rel_ahead(n, m, q, c, win):
                build_first(R, c, n, q)

            def rel_cycle(n, m, q, c, win):
                rest = pre[q][:, :].rearrange("p (u d) -> p u d", d=D)
                w0, w1 = win[0]
                dve.wait_ge(R["hi_done"], n + 1)
                dve.wait_ge(R["lo_done"], n + 1)
                nc.vector.tensor_tensor(rest, gath[q][:, :, :], m3[q][:, :, 0:D],
                                        ALU.subtract).then_inc(R["rest_done"], 1)
                if -1 in win:
                    add_first(R, visits_r, n - 1, 1 - q, win[-1][0])
                dve.wait_ge(R["mid_done"], n + 1)
                nc.vector.tensor_tensor(m3[q][:, :, 2 * D:], rest, m3[q][:, :, D:2 * D],
                                        ALU.subtract).then_inc(R["lo_done"], 1)
                add_extra(R, visits_r, c, n, q, w0, w1)

            def rel_end(n, m, q, c, win):
                add_first(R, visits_r, n, q, win[0][0])

            def stage_h(r, j, s):
                a, b = HALF[s]
                dve.wait_ge(hT_done, 2 * (r * NG + j) + s + 1)
                nc.vector.tensor_copy(stage_rows[:, a:b, :], agg[:, ds(j * GROUP + a, b - a), :]
                                      ).then_inc(h_staged, 1)

            with dve.Fori(0, RLAYERS) as r:
                dve.wait_ge(R["agg_added"], r * NCH + 2)
                carry_wait(dve)

                def each(j, more):
                    for s, (a, b) in enumerate(HALF):
                        if more:
                            stage_h(r, j + 1, s)
                        dve.wait_ge(self_done, 2 * (r * NG + j) + s + 1)
                        nc.vector.tensor_tensor(agg[:, ds(j * GROUP + a, b - a), :],
                                                sums[s][:, 0:(b - a) * D].rearrange("p (w d) -> p w d", d=D),
                                                bias_bc[:, ds(r, 1), :].to_broadcast([P, b - a, D]),
                                                ALU.add).then_inc(self_added, 1)

                steps(dve, lambda: [stage_h(r, 0, s) for s in range(2)], each)
                dve.wait_ge(self_added, 2 * (r + 1) * NG + 2)
                pipeline(dve, r, rel_ahead, rel_cycle, rel_end)
            dve.wait_ge(R["agg_added"], RLAYERS * NCH + 2)
            nc.vector.tensor_tensor(xres[:, :, :], xres[:, :, :], agg[:, :, :], ALU.add).then_inc(x3_added, 1)
            dve.wait_ge(x3_added, NG + 2)
            layer_norm(1, None)


LN_STEPS = 13
_OUT = ((6250, D), "float32")


def layouts(x, src, dst, edge_attr_16, edge_type_8, **rest):
    import numpy as np
    n, e = x.shape[0], len(src)
    rows = -(-n // (P * GROUP)) * (P * GROUP)
    if rows == n:
        rows += P * GROUP
    edges = -(-e // (2 * CHUNK)) * (2 * CHUNK)

    def fill(a, length, value):
        to = np.full((length, *a.shape[1:]), value, a.dtype)
        to[:len(a)] = a
        return to

    xp = fill(np.asarray(x), rows, 0)
    s, d, t = (fill(np.asarray(a), edges, v) for a, v in ((src, 0), (dst, n), (edge_type_8, 0)))
    attr = fill(np.asarray(edge_attr_16), edges, 0)
    cols = [np.ascontiguousarray(a.reshape(-1, P).T) for a in (s, d, t)]
    arrays = {"xT": np.ascontiguousarray(xp.T), "x_rows": xp, "src": cols[0], "dst": cols[1], "etype": cols[2],
              "dst_rows": d.reshape(-1, CHUNK),
              "edge_attr": np.ascontiguousarray(attr.reshape(-1, TILES, P, attr.shape[1]).transpose(0, 1, 3, 2)
                                           .reshape(edges // CHUNK, -1, P))}
    for k in ("msg_w", "msg_b", "upd_w", "upd_b"):
        arrays[k] = np.ascontiguousarray(rest["L0_gnn_" + k])
    for r in "12":
        for k in ("bases", "coef", "wself", "bias"):
            arrays[k + r] = np.ascontiguousarray(rest["L1_gnn_" + k + r])
    return arrays


def kernel(**inputs):
    import numpy as np
    import concourse.bacc as bacc
    from concourse.bass_utils import run_bass_kernel_spmd

    arrays = layouts(**inputs)
    nc = bacc.Bacc("TRN2", target_bir_lowering=False, num_devices=1)
    args = [nc.dram_tensor("in_" + k, a.shape, mybir.dt.from_np(a.dtype), kind="ExternalInput").ap()
            for k, a in arrays.items()]
    out = nc.dram_tensor("out", _OUT[0], mybir.dt.from_np(np.dtype(_OUT[1])), kind="ExternalOutput").ap()
    gnn_kernel(nc, *args, out)
    r = run_bass_kernel_spmd(nc, [{"in_" + k: a for k, a in arrays.items()}], core_ids=[0])
    return r.results[0]["out"]
```

```python
import concourse.bass as bass
from concourse import mybir
from contextlib import ExitStack

F32 = mybir.dt.float32
BF16 = mybir.dt.bfloat16
I32 = mybir.dt.int32
ALU = mybir.AluOpType
ACT = mybir.ActivationFunctionType
AX = mybir.AxisListType

P = 128
D = 64
TILES = 8
CHUNK = P * TILES
BUFFERS = 4
GROUP = 7
SPLIT = 4
EPS = 1e-5


def gnn_kernel(nc, xT, x_rows, src, dst, etype, dst_rows, edge_attr,
               msg_w, msg_b, upd_w, upd_b,
               bases1, coef1, wself1, bias1, bases2, coef2, wself2, bias2, out):
    NP = xT.shape[1]
    NW = NP // P
    NG = NW // GROUP
    NCH = edge_attr.shape[0]
    NE = edge_attr.shape[1] // TILES
    LAYERS = msg_w.shape[0]
    RLAYERS = 2
    NB, NR = coef1.shape[1], coef1.shape[0]
    PAIRS = NCH // 2
    QUADS = NCH // BUFFERS
    GN = GROUP * P
    SEG = PAIRS // NG
    assert SEG > 3
    READY_STEPS = 2 + NG
    HALF = [(0, SPLIT), (SPLIT, GROUP)]
    NORM_STEPS = 13
    LATE = 3 + LAYERS + 4 * RLAYERS
    LOADED = 16 * (4 + 3 * LAYERS)
    ds = bass.ds

    with ExitStack() as ctx:
        def sb(name, shape, dt):
            return ctx.enter_context(nc.sbuf_tensor(name, shape, dt))

        def pb(name, shape, dt=F32):
            return ctx.enter_context(nc.psum_tensor(name, shape, dt))

        def sem(name):
            return ctx.enter_context(nc.semaphore(name))

        msg_table = [nc.dram_tensor(f"msg_table{h}", [NP, D], F32).ap() for h in range(2)]
        rel_table = [nc.dram_tensor(f"rel_table{h}", [NP * NR, D], F32).ap() for h in range(2)]
        range_dram = nc.dram_tensor("range_dram", [NCH, 2], I32).ap()
        base_dram = nc.dram_tensor("base_dram", [NCH], F32).ap()

        src_sb = sb("src_sb", [P, NCH * TILES], I32)
        rel_sb = sb("rel_sb", [P, NCH * TILES], I32)
        dst_sb = sb("dst_sb", [P, NCH * TILES], I32)
        dst_rel = sb("dst_rel", [P, NCH * TILES], F32)
        base_bc = sb("base_bc", [P, NCH], F32)
        extreme = sb("extreme", [PAIRS, 2, 2], I32)
        window_range = sb("window_range", [PAIRS, 2, 2], I32)
        window_base = sb("window_base", [PAIRS, 2], F32)
        range_row = sb("range_row", [1, 2 * NCH], I32)
        ready_row = sb("ready_row", [1, NG], I32)
        ready_min = sb("ready_min", [1, NG], I32)
        group_end = sb("group_end", [1, NG], I32)
        window_start = sb("window_start", [P, NW], F32)
        x_relA = sb("x_relA", [P, TILES], F32)
        x_relB = sb("x_relB", [P, TILES], F32)
        col_id = sb("col_id", [P, P], I32)
        start_id = sb("start_id", [P, NW], I32)
        ident_f = sb("ident_f", [P, P], F32)
        ident_b = sb("ident_b", [P, P], BF16)
        eps_col = sb("eps_col", [P, 1], F32)

        xaT = sb("xaT", [P, NP], F32)
        a3 = sb("a3", [P, NW, 3 * D], BF16)
        b_rows = sb("b_rows", [P, NW, D], F32)
        agg = sb("agg", [P, NW, D], F32)
        xres = sb("xres", [P, NW, D], F32)

        w_ij_all = sb("w_ij_all", [D, LAYERS, 2 * D], F32)
        w_e_diag = sb("w_e_diag", [TILES * NE, LAYERS, TILES * D], F32)
        b_msg = sb("b_msg", [1, LAYERS, GROUP, D], F32)
        ones = sb("ones", [1, P], F32)
        w_upd_all = sb("w_upd_all", [P, LAYERS, D], F32)
        b_upd_all = sb("b_upd_all", [D, LAYERS], F32)
        w_ij = sb("w_ij", [D, 2 * D], F32)
        w_upd = sb("w_upd", [P, D], F32)
        b_upd = sb("b_upd", [D, 1], F32)
        bases = sb("bases", [D, RLAYERS, NB, D], F32)
        coef = sb("coef", [D, RLAYERS, NR, NB], F32)
        w_rel = sb("w_rel", [D, RLAYERS, NR * D + D], F32)
        w_tmp = sb("w_tmp", [D, NR, D], F32)
        bias_bc = sb("bias_bc", [P, RLAYERS, D], F32)

        idx = [sb(f"idx{b}", [P, TILES], I32) for b in range(BUFFERS)]
        attr = [sb(f"attr{q}", [TILES * NE, P], F32) for q in range(2)]
        gath = sb("gath", [P, BUFFERS * TILES, D], F32)
        hot = [sb(f"hot{q}", [P, TILES, P], BF16) for q in range(2)]
        hotT = sb("hotT", [P, TILES, P], BF16)
        x_hotA = sb("x_hotA", [P, TILES, P], BF16)
        x_hotT = sb("x_hotT", [P, TILES, P], BF16)
        x_hotB = sb("x_hotB", [P, TILES, P], BF16)
        m3 = [sb(f"m3_{q}", [P, TILES, 3 * D], BF16) for q in range(2)]
        part = sb("part", [P, D], F32)
        x_part = sb("x_part", [P, D], F32)

        stage_T = sb("stage_T", [D, GN], F32)
        stage_rows = sb("stage_rows", [P, GROUP, D], F32)
        a_rest = sb("a_rest", [P, GROUP, D], F32)
        rel_buffer = sb("rel_buffer", [P, GROUP, NR * D], F32)
        rel_rows = [rel_buffer[:, k, :] for k in range(GROUP)]
        chunk_dst = rel_buffer[0:PAIRS, :, :].rearrange("p k d -> p (k d)")[:, 0:2 * CHUNK].bitcast(I32) \
            .rearrange("p (a e) -> p a e", a=2)
        zeros = sb("zeros", [P, GROUP, D], F32)
        squares = sb("squares", [P, GROUP, D], F32)
        mean = sb("mean", [P, GROUP], F32)
        var = sb("var", [P, GROUP], F32)
        rstd = sb("rstd", [P, GROUP], F32)
        newton = sb("newton", [P, GROUP], F32)

        hotT_ps = pb("hotT_ps", [P, TILES, P], BF16)
        x_hotT_ps = pb("x_hotT_ps", [P, TILES, P], BF16)
        pre = [pb(f"pre{q}", [P, TILES * D]) for q in range(2)]
        sums = [pb(f"sums{q}", [P, TILES * D]) for q in range(2)]
        x_sums = pb("x_sums", [P, TILES * D])
        col_ps = pb("col_ps", [P, P])
        T_ps = [pre[0][:, :], hotT_ps[:, :, :].rearrange("p a b -> p (a b)").bitcast(F32)]
        upd_ps = [sums[1][:, :], x_hotT_ps[:, :, :].rearrange("p a b -> p (a b)").bitcast(F32)]
        rows_ps = x_sums[:, 0:GROUP * D].rearrange("p (w d) -> p w d", d=D)
        a_ps = pre[0][:, 0:GROUP * D].rearrange("p (w d) -> p w d", d=D)
        rel_ps = [T_ps[0], T_ps[1], upd_ps[0]]

        loaded = sem("loaded")
        late_loaded = sem("late_loaded")
        diag_loaded = sem("diag_loaded")
        range_made = sem("range_made")
        range_stored = sem("range_stored")
        range_loaded = sem("range_loaded")
        const_pool = sem("const_pool")
        setup_dve = sem("setup_dve")

        def chunk_sems(k):
            names = ["hot_built", "rows_ready", "z_done", "hi_done", "rest_done", "mid_done", "lo_done", "sums_done",
                     "part_done", "agg_added", "hotT_done", "hotT_copied", "pre_done",
                     "xa_rel", "xa_built", "xa_T", "xa_copied", "xb_rel", "xb_built", "xb_sums", "xb_part", "xb_added"]
            s = {n: sem(f"{k}_{n}") for n in names}
            s["attr_loaded"] = [sem(f"{k}_attr_loaded{q}") for q in range(2)]
            for n in ["idx_loaded", "gathered"]:
                s[n] = [sem(f"{k}_{n}{b}") for b in range(BUFFERS)]
            return s

        M = chunk_sems("msg")
        R = chunk_sems("rel")
        agg_zeroed = sem("agg_zeroed")
        xT_staged = sem("xT_staged")
        b_done = sem("b_done")
        ab_done = sem("ab_done")
        b_copied = sem("b_copied")
        a_hi = sem("a_hi")
        a_rested = sem("a_rested")
        a_mid = sem("a_mid")
        a_lo = sem("a_lo")
        x_kept = sem("x_kept")
        msg_stored = sem("msg_stored")
        weights_set = sem("weights_set")
        rel_weights = sem("rel_weights")
        rel_rows_made = sem("rel_rows_made")
        ready_made = sem("ready_made")
        agg_staged = sem("agg_staged")
        aggT_done = sem("aggT_done")
        aggT_copied = sem("aggT_copied")
        upd_done = sem("upd_done")
        x_updated = sem("x_updated")
        x3_rows = sem("x3_rows")
        norm = sem("norm")
        var_done = sem("var_done")
        std_done = sem("std_done")
        h_staged = sem("h_staged")
        hT_done = sem("hT_done")
        hT_copied = sem("hT_copied")
        rel_done = sem("rel_done")
        rel_copied = sem("rel_copied")
        rel_stored = sem("rel_stored")
        self_done = sem("self_done")
        self_added = sem("self_added")
        out_stored = sem("out_stored")
        carried = sem("carried")

        block = ctx.enter_context(nc.Block())

        def pipeline(eng, rnd, ahead, cycle, end=None, front=None, ranges=True, steps=(), settle=None):
            STEPS = len(steps)

            def at(step, i, k, win):
                step(rnd * NCH + 2 * i + k, rnd * PAIRS + i + k // 2, k % 2, 2 * i + k, win)

            def whole(i, k, first=False, last=False):
                c, before, after = 2 * i + k, 0 if first else 1, 0 if last else 1
                w = windows(eng, c - before, 1 + before + after) if ranges else []
                pairs = [tuple(w[2 * x:2 * x + 2]) for x in range(len(w) // 2)]
                if front is not None:
                    at(front, i, k, {})
                if not last:
                    at(ahead, i, k + 1, {x - before - 1: v for x, v in enumerate(pairs)})
                at(cycle, i, k, {x - before: v for x, v in enumerate(pairs)})
                if last and end is not None:
                    at(end, i, k, {x - before: v for x, v in enumerate(pairs)})

            def pair(i):
                whole(i, 1)
                whole(i, 2)

            at(ahead, 0, 0, {0: tuple(windows(eng, 0, 1))} if ranges else {})
            whole(0, 0, first=True)
            if STEPS:
                with eng.Fori(0, STEPS) as i:
                    pair(i)
                with eng.Fori(1, NG) as g:
                    with eng.Fori(g * SEG - SEG + STEPS, g * SEG) as i:
                        pair(i)
                    for x, step in enumerate(steps):
                        i = g * SEG + x
                        pair(i)
                        with eng.If(is_ready(eng, g - 1) > 0):
                            if settle is not None:
                                settle(rnd * NCH + 2 * i + 1)
                            step(g - 1)
            with eng.Fori((NG - 1) * SEG + STEPS if STEPS else 0, PAIRS - 1) as i:
                pair(i)
            whole(PAIRS - 1, 1, last=True)
            if STEPS:
                if settle is not None:
                    settle(rnd * NCH + NCH - 1)
                with eng.Fori(0, NG) as g:
                    with eng.If(is_ready(eng, g) < 1):
                        for step in steps:
                            step(g)

        def is_ready(eng, j):
            return nc.values_load_multi_w_load_instructions(
                ready_row[0:1, ds(j, 1)], engines=(eng.engine,), min_val=0, max_val=1,
                skip_runtime_bounds_check_because="it is the result of a comparison")[1][0]

        def count_in(eng, name):
            reg = eng.alloc_register(name)
            eng.reg_mov(reg, 0)
            return reg

        def settled(eng, S, visits):
            def settle(n):
                k = eng.snap(visits, min_val=0)
                eng.wait_ge(S["xb_added"], k + 1)
                carry_wait(eng)
                eng.wait_ge(S["agg_added"], n + 3)
                carry_wait(eng)
            return settle

        def carry_wait(eng):
            eng.sem_inc(carried, 1)

        def windows(eng, c, count):
            return nc.values_load_multi_w_load_instructions(
                range_row[0:1, ds(2 * c, 2 * count)], engines=(eng.engine,), min_val=0, max_val=NW - 1,
                skip_runtime_bounds_check_because="the destinations are nodes")[1]

        @block.sync
        def _(sp):
            sp.dma_start(chunk_dst[:, :, :], dst_rows.rearrange("(p a) e -> p a e", a=2)).then_inc(loaded, 16)
            sp.dma_start(dst_sb[:, :], dst).then_inc(loaded, 16)
            sp.dma_start(xaT[0:D, :], xT).then_inc(loaded, 16)
            sp.dma_start(src_sb[:, :], src).then_inc(loaded, 16)
            for l in range(LAYERS):
                sp.dma_start(w_ij_all[:, l, 0:D], msg_w[l, 0:D, :]).then_inc(loaded, 16)
                sp.dma_start(w_ij_all[:, l, D:], msg_w[l, D:2 * D, :]).then_inc(loaded, 16)
            for l in range(LAYERS):
                sp.dma_start(b_msg[:, l, :, :], msg_b[l:l + 1, :].unsqueeze(1).to_broadcast([1, GROUP, D])
                             ).then_inc(loaded, 16)
            sp.wait_ge(const_pool, 1)
            for u in range(TILES):
                sp.dma_start(w_e_diag[u * NE:(u + 1) * NE, :, u * D:(u + 1) * D],
                             msg_w[:, 2 * D:2 * D + NE, :].rearrange("l i o -> i l o")).then_inc(diag_loaded, 16)
            late = [(w_upd_all[:, :, :], upd_w.rearrange("l i o -> i l o")),
                    (rel_sb[:, :], etype),
                    (xres[:, :, :], x_rows.rearrange("(w p) d -> p w d", p=P))]
            late += [(b_upd_all[:, l:l + 1], upd_b[l, :].unsqueeze(1)) for l in range(LAYERS)]
            for r, (ba, co, ws, bi) in enumerate([(bases1, coef1, wself1, bias1),
                                                  (bases2, coef2, wself2, bias2)]):
                late += [(bases[:, r, :, :], ba.rearrange("b i o -> i b o")),
                         (coef[:, r, :, :], co.unsqueeze(0).to_broadcast([D, NR, NB])),
                         (w_rel[:, r, NR * D:], ws),
                         (bias_bc[:, r, :], bi.unsqueeze(0).to_broadcast([P, D]))]
            assert len(late) == LATE
            for to, of in late:
                sp.dma_start(to, of).then_inc(late_loaded, 16)
            sp.wait_ge(range_made, 4)
            sp.dma_start(range_dram.rearrange("(p a) b -> p (a b)", a=2),
                         window_range[:, :, :].rearrange("p a b -> p (a b)")).then_inc(range_stored, 16)
            sp.dma_start(base_dram.rearrange("(p a) -> p a", a=2), window_base[:, :]).then_inc(range_stored, 16)
            sp.wait_ge(range_stored, 32)
            sp.dma_start(range_row[:, :], range_dram.rearrange("(o c) b -> o (c b)", o=1)).then_inc(range_loaded, 16)
            sp.dma_start(base_bc[:, :], base_dram.unsqueeze(0).to_broadcast([P, NCH])).then_inc(range_loaded, 16)


            def load_indices(S, c, b, rows):
                sp.dma_start(idx[b][:, :], rows[:, ds(c * TILES, TILES)]).then_inc(S["idx_loaded"][b], 16)

            def load_attributes(c, n, q):
                sp.wait_ge(M["pre_done"], n + 1)
                sp.dma_start(attr[q][:, :], edge_attr[ds(c, 1), :, :].rearrange("a f e -> (a f) e")
                             ).then_inc(M["attr_loaded"][q], 16)

            def chunks(S, rnd, rows, following):
                def gathered(i, b):
                    sp.wait_ge(S["gathered"][b], 16 * TILES * (rnd * QUADS + i + 1))
                    sp.sem_inc(S["rows_ready"], 1)

                with sp.Fori(0, QUADS - 1) as i:
                    for b in range(BUFFERS):
                        c = BUFFERS * i + b
                        gathered(i, b)
                        load_indices(S, c + BUFFERS, b, rows)
                        if S is M:
                            load_attributes(c + 2, rnd * NCH + c + 2, b % 2)
                for b in range(BUFFERS):
                    c = NCH - BUFFERS + b
                    gathered(QUADS - 1, b)
                    if following is not None:
                        load_indices(following[0], b, b, following[1])
                    if S is M and c + 2 < NCH:
                        load_attributes(c + 2, rnd * NCH + c + 2, b % 2)
                    elif S is M and following[0] is M:
                        load_attributes(c + 2 - NCH, rnd * NCH + c + 2, b % 2)

            for b in range(BUFFERS):
                load_indices(M, b, b, src_sb)
            for q in range(2):
                load_attributes(q, q, q)
            with sp.Fori(0, LAYERS - 1) as l:
                chunks(M, l, src_sb, (M, src_sb))
            sp.wait_ge(rel_rows_made, 1)
            chunks(M, LAYERS - 1, src_sb, (R, rel_sb))
            with sp.Fori(0, RLAYERS - 1) as r:
                chunks(R, r, rel_sb, (R, rel_sb))
            chunks(R, RLAYERS - 1, rel_sb, None)
            sp.wait_ge(out_stored, 16 * NG)

        @block.gpsimd
        def _(pool):
            pool.memset(w_e_diag[:, :, :], 0.0).then_inc(const_pool, 1)
            pool.iota(col_id[:, :], [[1, P]], base=0, channel_multiplier=0).then_inc(const_pool, 1)
            pool.memset(ones[:, :], 1.0).then_inc(const_pool, 1)
            pool.memset(ident_f[:, :], 0.0).then_inc(const_pool, 1)
            pool.memset(eps_col[:, :], EPS).then_inc(const_pool, 1)
            pool.wait_ge(const_pool, 5)
            pool.affine_select(ident_f[:, :], ident_f[:, :], [[-1, P]], ALU.not_equal, 1.0, base=0,
                               channel_multiplier=1).then_inc(const_pool, 1)
            pool.iota(start_id[:, :], [[P, NW]], base=0, channel_multiplier=0).then_inc(const_pool, 1)
            pool.iota(group_end[:, :], [[GROUP, NG]], base=GROUP, channel_multiplier=0).then_inc(const_pool, 1)

            def gather(S, table, rnd, i, b, used):
                pool.wait_ge(S["idx_loaded"][b], 16 * (rnd * QUADS + i + 1))
                pool.wait_ge(S[used], rnd * NCH + BUFFERS * i + b + 1)
                carry_wait(pool)
                for u in range(TILES):
                    pool.indirect_dma_start(gath[:, b * TILES + u, :], None, table,
                                            bass.IndirectOffsetOnAxis(ap=idx[b][:, u:u + 1], axis=0)
                                            ).then_inc(S["gathered"][b], 16)

            for l in range(LAYERS):
                pool.wait_ge(msg_stored, 16 * NG * (l + 1))
                with pool.Fori(0, QUADS) as i:
                    for b in range(BUFFERS):
                        gather(M, msg_table[l % 2], l, i, b, "z_done")
            for r in range(RLAYERS):
                pool.wait_ge(rel_stored, 16 * NW * (r + 1))
                with pool.Fori(0, QUADS) as i:
                    for b in range(BUFFERS):
                        gather(R, rel_table[r % 2], r, i, b, "rest_done")

        @block.scalar
        def _(act):
            visits = act.alloc_register("act_visits")
            act.reg_mov(visits, 0)
            act.sem_inc(M["hotT_copied"], 1)
            updates, norms, rels = (count_in(act, "act_" + name) for name in ("updates", "norms", "rels"))

            def msg_ahead(n, m, q, c, win):
                w0, w1 = win[0]
                act.wait_ge(M["hotT_done"], n + 1)
                act.activation(hotT[:, :, :], hotT_ps[:, :, :], ACT.Copy).then_inc(M["hotT_copied"], 1)
                with act.If(w0 < w1):
                    with act.Fori(w0, w1):
                        k = act.snap(visits, min_val=0)
                        act.wait_ge(M["xa_T"], k + 2)
                        act.activation(x_hotT[:, :, :], x_hotT_ps[:, :, :], ACT.Copy).then_inc(M["xa_copied"], 1)
                        act.reg_add(visits, visits, 1)

            def msg_front(n, m, q, c, win):
                z = pre[q][:, :].rearrange("p (u d) -> p u d", d=D)
                act.wait_ge(M["z_done"], n + BUFFERS + 1)
                act.wait_ge(M["sums_done"], n + 1)
                act.activation(m3[q][:, :, 0:D], z, ACT.Relu).then_inc(M["hi_done"], 1)

            def msg_cycle(n, m, q, c, win):
                z = pre[q][:, :].rearrange("p (u d) -> p u d", d=D)
                act.wait_ge(M["rest_done"], n + 1)
                act.activation(m3[q][:, :, D:2 * D], z, ACT.Copy).then_inc(M["mid_done"], 1)

            def msg_tables(l, t, j):
                act.wait_ge(b_done, t + 1)
                act.activation(b_rows[:, ds(j * GROUP, GROUP), :], rows_ps, ACT.Copy).then_inc(b_copied, 1)
                act.wait_ge(b_copied, t + 1)

                def store(h):
                    act.dma_start(msg_table[h][ds(j * GN, GN), :].rearrange("(w p) d -> p w d", p=P),
                                  b_rows[:, ds(j * GROUP, GROUP), :]).then_inc(msg_stored, 16)

                if l is None:
                    store(0)
                else:
                    for h in range(2):
                        with act.If(l % 2 < 1 if h == 0 else l % 2 > 0):
                            store(h)
                act.wait_ge(ab_done, t + 2)
                act.activation(a3[:, ds(j * GROUP, GROUP), 0:D], a_ps, ACT.Copy).then_inc(a_hi, 1)
                act.wait_ge(a_rested, t + 1)
                act.activation(a3[:, ds(j * GROUP, GROUP), D:2 * D], a_rest[:, :, :], ACT.Copy).then_inc(a_mid, 1)

            def update(t, j):
                for s, (a, b) in enumerate(HALF):
                    act.wait_ge(aggT_done, 2 * t + s + 1)
                    act.activation(xaT[D:2 * D, ds(j * GN + a * P, (b - a) * P)],
                                   T_ps[s][0:D, 0:(b - a) * P], ACT.Copy).then_inc(aggT_copied, 1)
                for s, (a, b) in enumerate(HALF):
                    act.wait_ge(upd_done, 2 * t + s + 1)
                    act.activation(stage_T[:, a * P:b * P], upd_ps[s][0:D, 0:(b - a) * P],
                                   ACT.Relu, bias=b_upd[:, :]).then_inc(x_updated, 1)

            def root(t):
                act.wait_ge(var_done, t + 1)
                act.activation(rstd[:, :], var[:, :], ACT.Sqrt, bias=eps_col[:, :]).then_inc(std_done, 1)

            act.wait_ge(loaded, LOADED)
            with act.Fori(0, NG) as j:
                act.wait_ge(ab_done, j + 1)
                act.activation(stage_T[:, :], xaT[0:D, ds(j * GN, GN)], ACT.Copy).then_inc(xT_staged, 1)
                msg_tables(None, j, j)
            act.wait_ge(late_loaded, 16 * LATE)
            act.wait_ge(ready_made, READY_STEPS)

            def set_weights(l):
                act.wait_ge(ab_done, (l + 1) * NG + 1)
                act.activation(w_upd[:, :], w_upd_all[:, ds(l, 1), :].rearrange("p a d -> p (a d)"),
                               ACT.Copy).then_inc(weights_set, 1)
                act.activation(b_upd[:, :], b_upd_all[:, ds(l, 1)], ACT.Copy).then_inc(weights_set, 1)

            def update_step(l, j):
                t = act.snap(updates, min_val=0)
                update(t, j)
                msg_tables(l + 1, t + NG, j)
                act.reg_add(updates, updates, 1)

            def norm_step(j):
                t = act.snap(norms, min_val=0)
                update(t + (LAYERS - 1) * NG, j)
                root(t)
                act.reg_add(norms, norms, 1)

            def rel_step(r, j, s):
                t = act.snap(rels, min_val=0)
                if s == 0:
                    for x, (a, b) in enumerate(HALF):
                        act.wait_ge(hT_done, 2 * t + x + 1)
                        act.activation(stage_T[:, a * P:b * P], T_ps[x][0:D, 0:(b - a) * P],
                                       ACT.Copy).then_inc(hT_copied, 1)
                    with act.If(t > 0):
                        act.wait_ge(rel_stored, t * GROUP * 16)
                        carry_wait(act)
                for k in range(*HALF[s]):
                    act.wait_ge(rel_done, t * GROUP + k + 1)
                    act.activation(rel_rows[k], rel_ps[k % 3], ACT.Copy).then_inc(rel_copied, 1)
                    act.wait_ge(rel_copied, t * GROUP + k + 1)
                    act.dma_start(rel_table[r % 2][ds((j * GROUP + k) * (P * NR), P * NR), :]
                                  .rearrange("(p a) d -> p (a d)", a=NR), rel_rows[k]).then_inc(rel_stored, 16)
                if s == 1:
                    act.reg_add(rels, rels, 1)

            with act.Fori(0, LAYERS - 1) as l:
                set_weights(l)
                act.activation(w_ij[:, :], w_ij_all[:, ds(l + 1, 1), :].rearrange("p a d -> p (a d)"),
                               ACT.Copy).then_inc(weights_set, 1)
                pipeline(act, l, msg_ahead, msg_cycle, front=msg_front, steps=[lambda j: update_step(l, j)])
            set_weights(LAYERS - 1)
            pipeline(act, LAYERS - 1, msg_ahead, msg_cycle, front=msg_front,
                     steps=[norm_step, lambda j: rel_step(0, j, 0), lambda j: rel_step(0, j, 1)])

            def rel_ahead(n, m, q, c, win):
                pass

            def rel_cycle(n, m, q, c, win):
                act.wait_ge(R["rows_ready"], n + 1)
                act.wait_ge(R["sums_done"], n + 1)
                act.activation(m3[q][:, :, 0:D], gath[:, ds((c % BUFFERS) * TILES, TILES), :], ACT.Copy).then_inc(R["hi_done"], 1)
                act.wait_ge(R["rest_done"], n + BUFFERS + 1)
                act.activation(m3[q][:, :, D:2 * D], pre[q][:, :].rearrange("p (u d) -> p u d", d=D),
                               ACT.Copy).then_inc(R["mid_done"], 1)

            def last_step(j):
                t = act.snap(norms, min_val=0)
                root(t)
                act.wait_ge(norm, NORM_STEPS * (t + 1))
                act.dma_start(out[ds(j * GN, GN), :].rearrange("(w p) d -> p w d", p=P),
                              xres[:, ds(j * GROUP, GROUP), :]).then_inc(out_stored, 16)
                act.reg_add(norms, norms, 1)

            for r in range(RLAYERS - 1):
                pipeline(act, r, rel_ahead, rel_cycle, ranges=False,
                         steps=[lambda j: rel_step(r + 1, j, 0), lambda j: rel_step(r + 1, j, 1)])
            pipeline(act, RLAYERS - 1, rel_ahead, rel_cycle, ranges=False, steps=[last_step])

        @block.tensor
        def _(pe):
            visits_a = pe.alloc_register("pe_visits_a")
            visits_b = pe.alloc_register("pe_visits_b")
            visits_r = pe.alloc_register("pe_visits_r")
            for reg in (visits_a, visits_b, visits_r):
                pe.reg_mov(reg, 0)
            pe.sem_inc(M["sums_done"], 2)
            pe.sem_inc(R["sums_done"], 2)
            pe.sem_inc(M["pre_done"], 2)
            pe.sem_inc(M["xa_T"], 1)
            pe.sem_inc(ab_done, 1)
            updates, norms, rels = (count_in(pe, "pe_" + name) for name in ("updates", "norms", "rels"))

            def transposes(to, of):
                for u in range(TILES):
                    last = nc.tensor.transpose(to[:, u, :], of[:, u, :], ident_b[:, :])
                return last

            def expand(to, of, w, stop):
                for u in range(TILES):
                    for k in range(3):
                        last = nc.tensor.matmul(to[:, u * D:(u + 1) * D], of[:, u, :],
                                                a3[:, ds(w, 1), k * D:(k + 1) * D].rearrange("p a d -> p (a d)"),
                                                start=False, stop=stop and k == 2 and u == TILES - 1)
                return last

            def sum_up(to, hots, parts):
                for u in range(TILES):
                    last = nc.tensor.matmul(to[:, 0:3 * D], hots[:, u, :], parts[:, u, :],
                                            start=u == 0, stop=u == TILES - 1)
                return last

            def msg_ahead(l, n, m, q, c, win):
                w0, w1 = win[0]
                pe.wait_ge(M["attr_loaded"][q], 16 * (m + 1))
                pe.wait_ge(M["lo_done"], n + 1)
                nc.tensor.matmul(pre[q][:, :], attr[q][:, :],
                                 w_e_diag[:, ds(l, 1), :].rearrange("p a d -> p (a d)"), start=True, stop=False)
                pe.wait_ge(M["hot_built"], n + 1)
                pe.wait_ge(M["hotT_copied"], n + 1)
                transposes(hotT_ps, hot[q]).then_inc(M["hotT_done"], 1)
                with pe.If(w0 < w1):
                    with pe.Fori(w0, w1) as w:
                        k = pe.snap(visits_a, min_val=0)
                        pe.wait_ge(M["xa_built"], k + 1)
                        transposes(x_hotT_ps, x_hotA).then_inc(M["xa_T"], 1)
                        pe.wait_ge(M["xa_copied"], k + 1)
                        expand(pre[q], x_hotT, w + 1, False)
                        pe.reg_add(visits_a, visits_a, 1)
                pe.wait_ge(M["hotT_copied"], n + 2)
                expand(pre[q], hotT, w0, True).then_inc(M["pre_done"], 1)

            def sums_cycle(S, visits):
                def run(n, m, q, c, win):
                    w0, w1 = win[0]
                    with pe.If(w0 < w1):
                        with pe.Fori(w0, w1):
                            k = pe.snap(visits, min_val=0)
                            pe.wait_ge(S["xb_built"], k + 1)
                            sum_up(x_sums, x_hotB, m3[q]).then_inc(S["xb_sums"], 1)
                            pe.reg_add(visits, visits, 1)
                    pe.wait_ge(S["agg_added"], n + 1)
                    pe.wait_ge(S["lo_done"], n + 3)
                    sum_up(sums[q], hot[q], m3[q]).then_inc(S["sums_done"], 1)
                return run

            def rel_ahead(n, m, q, c, win):
                pe.wait_ge(R["hot_built"], n + 1)
                carry_wait(pe)

            def msg_tables(t, weights, bias):
                for w in range(GROUP):
                    last = nc.tensor.matmul(x_sums[:, w * D:(w + 1) * D], stage_T[:, w * P:(w + 1) * P],
                                            weights[:, D:2 * D], start=True, stop=True)
                last.then_inc(b_done, 1)
                nc.tensor.matmul(pre[0][:, 0:GROUP * D], ones[:, :], bias, start=True, stop=False)
                for w in range(GROUP):
                    last = nc.tensor.matmul(pre[0][:, w * D:(w + 1) * D], stage_T[:, w * P:(w + 1) * P],
                                            weights[:, 0:D], start=False, stop=w == GROUP - 1)
                last.then_inc(ab_done, 1)
                pe.wait_ge(b_copied, t + 1)
                pe.wait_ge(a_lo, t + 2)

            def transpose_rows(done):
                for s, (a, b) in enumerate(HALF):
                    for w in range(a, b):
                        last = nc.tensor.transpose(T_ps[s][0:D, (w - a) * P:(w - a + 1) * P],
                                                   stage_rows[:, w, :], ident_f[:, :])
                    last.then_inc(done, 1)

            def update(t, j):
                pe.wait_ge(agg_staged, t + 1)
                carry_wait(pe)
                transpose_rows(aggT_done)
                for s, (a, b) in enumerate(HALF):
                    pe.wait_ge(aggT_copied, 2 * t + s + 1)
                    nc.tensor.matmul(upd_ps[s][0:D, 0:(b - a) * P], w_upd[:, :],
                                     xaT[:, ds(j * GN + a * P, (b - a) * P)],
                                     start=True, stop=True).then_inc(upd_done, 1)
                pe.wait_ge(x_updated, 2 * t + 2)

            def update_step(l, j):
                t = pe.snap(updates, min_val=0)
                update(t, j)
                msg_tables(t + NG, w_ij, b_msg[:, ds(l + 1, 1), :, :].rearrange("p a w d -> p (a w d)"))
                pe.wait_ge(x_kept, t + 1)
                carry_wait(pe)
                pe.reg_add(updates, updates, 1)

            def norm_step(j):
                t = pe.snap(norms, min_val=0)
                update(t + (LAYERS - 1) * NG, j)
                carry_wait(pe)
                for w in range(GROUP):
                    last = nc.tensor.transpose(x_sums[:, w * D:(w + 1) * D], stage_T[:, w * P:(w + 1) * P],
                                               ident_f[0:D, 0:D])
                last.then_inc(x3_rows, 1)
                pe.wait_ge(norm, NORM_STEPS * t + 1)
                carry_wait(pe)
                pe.reg_add(norms, norms, 1)

            def rel_step(r, j, s):
                t = pe.snap(rels, min_val=0)
                if s == 0:
                    pe.wait_ge(h_staged, t + 1)
                    carry_wait(pe)
                    transpose_rows(hT_done)
                    pe.wait_ge(hT_copied, 2 * t + 2)
                    carry_wait(pe)
                a, b = HALF[s]
                for k in range(a, b):
                    if k >= a + 3:
                        pe.wait_ge(rel_copied, t * GROUP + k - 2)
                        carry_wait(pe)
                    nc.tensor.matmul(rel_ps[k % 3], stage_T[:, k * P:(k + 1) * P],
                                     w_rel[:, ds(r, 1), 0:NR * D].rearrange("p a d -> p (a d)"),
                                     start=True, stop=True).then_inc(rel_done, 1)
                for k in range(a, b):
                    last = nc.tensor.matmul(x_sums[:, k * D:(k + 1) * D], stage_T[:, k * P:(k + 1) * P],
                                            w_rel[:, ds(r, 1), NR * D:].rearrange("p a d -> p (a d)"),
                                            start=True, stop=True)
                last.then_inc(self_done, 1)
                pe.wait_ge(rel_copied, t * GROUP + b)
                pe.wait_ge(self_added, 2 * t + s + 1)
                carry_wait(pe)
                if s == 1:
                    pe.reg_add(rels, rels, 1)

            pe.wait_ge(setup_dve, 1)
            pe.wait_ge(const_pool, 8)
            with pe.Fori(0, NG) as j:
                pe.wait_ge(xT_staged, j + 1)
                msg_tables(j, w_ij_all[:, 0, :], b_msg[:, 0, :, :].rearrange("p w d -> p (w d)"))
            with pe.Fori(0, LAYERS - 1) as l:
                pe.wait_ge(weights_set, 3 * (l + 1))
                carry_wait(pe)
                pe.wait_ge(ready_made, READY_STEPS)
                pe.wait_ge(diag_loaded, 16 * TILES)
                pipeline(pe, l, lambda *at: msg_ahead(l, *at), sums_cycle(M, visits_b),
                         settle=settled(pe, M, visits_b), steps=[lambda j: update_step(l, j)])
            pe.wait_ge(weights_set, 3 * LAYERS - 1)
            pipeline(pe, LAYERS - 1, lambda *at: msg_ahead(LAYERS - 1, *at), sums_cycle(M, visits_b),
                     settle=settled(pe, M, visits_b),
                     steps=[norm_step, lambda j: rel_step(0, j, 0), lambda j: rel_step(0, j, 1)])
            for r in range(RLAYERS - 1):
                pipeline(pe, r, rel_ahead, sums_cycle(R, visits_r), settle=settled(pe, R, visits_r),
                         steps=[lambda j: rel_step(r + 1, j, 0), lambda j: rel_step(r + 1, j, 1)])
            pipeline(pe, RLAYERS - 1, rel_ahead, sums_cycle(R, visits_r))

        @block.vector
        def _(dve):
            visits_a = dve.alloc_register("dve_visits_a")
            visits_b = dve.alloc_register("dve_visits_b")
            visits_r = dve.alloc_register("dve_visits_r")
            for reg in (visits_a, visits_b, visits_r):
                dve.reg_mov(reg, 0)
            for S in (M, R):
                dve.sem_inc(S["lo_done"], 2)
                dve.sem_inc(S["agg_added"], 2)
                dve.sem_inc(S["xb_added"], 1)
            dve.sem_inc(M["z_done"], BUFFERS)
            dve.sem_inc(R["rest_done"], BUFFERS)
            dve.sem_inc(a_lo, 1)
            updates, norms, rels = (count_in(dve, "dve_" + name) for name in ("updates", "norms", "rels"))

            dve.wait_ge(const_pool, 8)
            nc.vector.tensor_copy(col_ps[:, :], col_id[:, :])
            nc.vector.tensor_copy(window_start[:, :], start_id[:, :])
            nc.vector.tensor_copy(ident_b[:, :], ident_f[:, :]).then_inc(setup_dve, 1)
            dve.wait_ge(loaded, LOADED)
            nc.vector.tensor_reduce(extreme[:, :, 0], chunk_dst[:, :, :], AX.X, ALU.min).then_inc(range_made, 1)
            nc.vector.tensor_reduce(extreme[:, :, 1], chunk_dst[:, :, :], AX.X, ALU.max).then_inc(range_made, 1)
            dve.wait_ge(range_made, 2)
            nc.vector.tensor_scalar(window_range[:, :, :], extreme[:, :, :], 7, None,
                                    ALU.arith_shift_right).then_inc(range_made, 1)
            dve.wait_ge(range_made, 3)
            nc.vector.tensor_scalar(window_base[:, :], window_range[:, :, 0], float(P), None,
                                    ALU.mult).then_inc(range_made, 1)
            cols = col_ps[:, :].unsqueeze(1).to_broadcast([P, TILES, P])

            def build_first(S, c, n, q):
                dve.wait_ge(S["sums_done"], n + 1)
                nc.vector.tensor_tensor(hot[q][:, :, :], cols,
                                        dst_rel[:, ds(c * TILES, TILES)].unsqueeze(2).to_broadcast([P, TILES, P]),
                                        ALU.is_equal).then_inc(S["hot_built"], 1)

            def build(to, rel, rel_made, done, k, c, w):
                nc.vector.tensor_tensor(rel[:, :], dst_sb[:, ds(c * TILES, TILES)],
                                        window_start[:, ds(w, 1)].to_broadcast([P, TILES]),
                                        ALU.subtract).then_inc(rel_made, 1)
                dve.wait_ge(rel_made, k + 1)
                nc.vector.tensor_tensor(to[:, :, :], cols, rel[:, :].unsqueeze(2).to_broadcast([P, TILES, P]),
                                        ALU.is_equal).then_inc(done, 1)

            def add_extra(S, visits, c, n, q, w0, w1):
                with dve.If(w0 < w1):
                    with dve.Fori(w0, w1) as w:
                        k = dve.snap(visits, min_val=0)
                        dve.wait_ge(S["xb_added"], k + 1)
                        dve.wait_ge(S["agg_added"], n + 2)
                        build(x_hotB, x_relB, S["xb_rel"], S["xb_built"], k, c, w + 1)
                        dve.wait_ge(S["xb_sums"], k + 1)
                        nc.vector.tensor_reduce(x_part[:, :], x_sums[:, 0:3 * D].rearrange("p (k d) -> p d k", d=D),
                                                AX.X, ALU.add).then_inc(S["xb_part"], 1)
                        dve.wait_ge(S["xb_part"], k + 1)
                        to = agg[:, ds(w + 1, 1), :].rearrange("p a d -> p (a d)")
                        nc.vector.tensor_tensor(to, to, x_part[:, :], ALU.add).then_inc(S["xb_added"], 1)
                        dve.reg_add(visits, visits, 1)

            def add_first(S, visits, n, q, w0):
                k = dve.snap(visits, min_val=0)
                dve.wait_ge(S["xb_added"], k + 1)
                dve.wait_ge(S["agg_added"], n + 2)
                dve.wait_ge(S["sums_done"], n + 3)
                nc.vector.tensor_reduce(part[:, :], sums[q][:, 0:3 * D].rearrange("p (k d) -> p d k", d=D),
                                        AX.X, ALU.add).then_inc(S["part_done"], 1)
                dve.wait_ge(S["part_done"], n + 1)
                to = agg[:, ds(w0, 1), :].rearrange("p a d -> p (a d)")
                nc.vector.tensor_tensor(to, to, part[:, :], ALU.add).then_inc(S["agg_added"], 1)

            def msg_ahead(n, m, q, c, win):
                w0, w1 = win[0]
                build_first(M, c, n, q)
                with dve.If(w0 < w1):
                    with dve.Fori(w0, w1) as w:
                        k = dve.snap(visits_a, min_val=0)
                        dve.wait_ge(M["xa_T"], k + 1)
                        build(x_hotA, x_relA, M["xa_rel"], M["xa_built"], k, c, w + 1)
                        dve.reg_add(visits_a, visits_a, 1)

            def msg_front(n, m, q, c, win):
                z = pre[q][:, :].rearrange("p (u d) -> p u d", d=D)
                dve.wait_ge(M["pre_done"], n + 3)
                dve.wait_ge(M["rows_ready"], n + 1)
                nc.vector.tensor_tensor(z, z, gath[:, ds((c % BUFFERS) * TILES, TILES), :], ALU.add).then_inc(M["z_done"], 1)

            def msg_cycle(n, m, q, c, win):
                z = pre[q][:, :].rearrange("p (u d) -> p u d", d=D)
                w0, w1 = win[0]
                if -1 in win:
                    add_first(M, visits_b, n - 1, 1 - q, win[-1][0])
                dve.wait_ge(M["hi_done"], n + 1)
                nc.vector.scalar_tensor_tensor(z, z, 0.0, m3[q][:, :, 0:D], ALU.max,
                                               ALU.subtract).then_inc(M["rest_done"], 1)
                dve.wait_ge(M["mid_done"], n + 1)
                nc.vector.tensor_tensor(m3[q][:, :, 2 * D:], z, m3[q][:, :, D:2 * D],
                                        ALU.subtract).then_inc(M["lo_done"], 1)
                add_extra(M, visits_b, c, n, q, w0, w1)

            def split_tables(t, j):
                to = a3[:, ds(j * GROUP, GROUP), :]
                dve.wait_ge(a_hi, t + 1)
                nc.vector.tensor_tensor(a_rest[:, :, :], a_ps, to[:, :, 0:D], ALU.subtract).then_inc(a_rested, 1)
                dve.wait_ge(a_mid, t + 1)
                nc.vector.tensor_tensor(to[:, :, 2 * D:], a_rest[:, :, :], to[:, :, D:2 * D],
                                        ALU.subtract).then_inc(a_lo, 1)

            def msg_end(n, m, q, c, win):
                add_first(M, visits_b, n, q, win[0][0])

            nc.vector.memset(zeros[:, :, :], 0.0).then_inc(agg_zeroed, 1)
            nc.vector.memset(agg[:, :, :], 0.0).then_inc(agg_zeroed, 1)
            with dve.Fori(0, NG) as j:
                split_tables(j, j)
            dve.wait_ge(range_loaded, 32)
            nc.vector.tensor_tensor(dst_rel[:, :].rearrange("p (c u) -> p c u", u=TILES),
                                    dst_sb[:, :].rearrange("p (c u) -> p c u", u=TILES),
                                    base_bc[:, :].unsqueeze(2).to_broadcast([P, NCH, TILES]),
                                    ALU.subtract).then_inc(ready_made, 1)
            nc.vector.memset(ready_min[:, :], 0).then_inc(ready_made, 1)
            dve.wait_ge(ready_made, 2)
            lows = range_row[:, :].rearrange("o (c b) -> o c b", b=2)
            for j in range(NG - 1):
                nc.vector.tensor_reduce(ready_min[:, j:j + 1], lows[:, 2 * ((j + 1) * SEG + 1):, 0], AX.X,
                                        ALU.min).then_inc(ready_made, 1)
            dve.wait_ge(ready_made, 1 + NG)
            nc.vector.tensor_tensor(ready_row[:, :], ready_min[:, :], group_end[:, :],
                                    ALU.is_ge).then_inc(ready_made, 1)
            dve.wait_ge(ready_made, READY_STEPS)

            dve.wait_ge(late_loaded, 16 * LATE)
            chain = 0
            for r in range(RLAYERS):
                w = w_rel[:, r, 0:NR * D].rearrange("p (r d) -> p r d", d=D)
                for b in range(NB):
                    to = w if b == 0 else w_tmp[:, :, :]
                    nc.vector.tensor_tensor(to, bases[:, r, b, :].unsqueeze(1).to_broadcast([D, NR, D]),
                                            coef[:, r, :, b].unsqueeze(2).to_broadcast([D, NR, D]),
                                            ALU.mult).then_inc(rel_weights, 1)
                    chain += 1
                    dve.wait_ge(rel_weights, chain)
                    if b:
                        nc.vector.tensor_tensor(w, w, w_tmp[:, :, :], ALU.add).then_inc(rel_weights, 1)
                        chain += 1
                        dve.wait_ge(rel_weights, chain)
            nc.vector.scalar_tensor_tensor(rel_sb[:, :], src_sb[:, :], float(NR), rel_sb[:, :],
                                           ALU.mult, ALU.add).then_inc(rel_rows_made, 1)
            def stage_agg(j, done):
                nc.vector.tensor_copy(stage_rows[:, :, :], agg[:, ds(j * GROUP, GROUP), :]).then_inc(done, 1)

            def update_step(l, j):
                t = dve.snap(updates, min_val=0)
                stage_agg(j, agg_staged)
                dve.wait_ge(x_updated, 2 * t + 2)
                nc.vector.tensor_copy(xaT[0:D, ds(j * GN, GN)], stage_T[:, :]).then_inc(x_kept, 1)
                nc.vector.tensor_copy(agg[:, ds(j * GROUP, GROUP), :], zeros[:, :, :]).then_inc(agg_zeroed, 1)
                split_tables(t + NG, j)
                dve.reg_add(updates, updates, 1)

            def layer_norm(t, j, more, copy_to):
                at = 0
                bc = [P, GROUP, D]
                x = xres[:, ds(j * GROUP, GROUP), :]

                def step(ins):
                    nonlocal at
                    at += 1
                    ins.then_inc(norm, 1)
                    dve.wait_ge(norm, t * NORM_STEPS + at)
                    carry_wait(dve)

                step(nc.vector.tensor_tensor(x, x, more, ALU.add))
                step(nc.vector.tensor_reduce(mean[:, :], x, AX.X, ALU.add))
                step(nc.vector.tensor_scalar(mean[:, :], mean[:, :], 1.0 / D, None, ALU.mult))
                step(nc.vector.tensor_tensor(x, x, mean[:, :].unsqueeze(2).to_broadcast(bc), ALU.subtract))
                step(nc.vector.tensor_tensor(squares[:, :, :], x, x, ALU.mult))
                step(nc.vector.tensor_reduce(var[:, :], squares[:, :, :], AX.X, ALU.add))
                nc.vector.tensor_scalar(var[:, :], var[:, :], 1.0 / D, None, ALU.mult).then_inc(var_done, 1)
                dve.wait_ge(std_done, t + 1)
                carry_wait(dve)
                step(nc.vector.reciprocal(rstd[:, :], rstd[:, :]))
                step(nc.vector.tensor_tensor(newton[:, :], rstd[:, :], rstd[:, :], ALU.mult))
                step(nc.vector.tensor_scalar(var[:, :], var[:, :], EPS, None, ALU.add))
                step(nc.vector.tensor_tensor(newton[:, :], newton[:, :], var[:, :], ALU.mult))
                step(nc.vector.tensor_scalar(newton[:, :], newton[:, :], -0.5, 1.5, ALU.mult, ALU.add))
                step(nc.vector.tensor_tensor(rstd[:, :], rstd[:, :], newton[:, :], ALU.mult))
                step(nc.vector.tensor_tensor(x, x, rstd[:, :].unsqueeze(2).to_broadcast(bc), ALU.mult))
                if copy_to is not None:
                    nc.vector.tensor_copy(copy_to, x).then_inc(h_staged, 1)
                assert at == NORM_STEPS

            def norm_step(j):
                t = dve.snap(norms, min_val=0)
                stage_agg(j, agg_staged)
                dve.wait_ge(x3_rows, t + 1)
                carry_wait(dve)
                layer_norm(t, j, rows_ps, stage_rows[:, :, :])
                dve.reg_add(norms, norms, 1)

            def rel_step(r, j, s, stage):
                t = dve.snap(rels, min_val=0)
                if stage:
                    stage_agg(j, h_staged)
                a, b = HALF[s]
                dve.wait_ge(self_done, 2 * t + s + 1)
                nc.vector.tensor_tensor(agg[:, ds(j * GROUP + a, b - a), :], rows_ps[:, a:b, :],
                                        bias_bc[:, ds(r, 1), :].to_broadcast([P, b - a, D]),
                                        ALU.add).then_inc(self_added, 1)
                if s == 1:
                    dve.reg_add(rels, rels, 1)

            def last_step(j):
                t = dve.snap(norms, min_val=0)
                layer_norm(t, j, agg[:, ds(j * GROUP, GROUP), :], None)
                dve.reg_add(norms, norms, 1)

            with dve.Fori(0, LAYERS - 1) as l:
                dve.wait_ge(agg_zeroed, l * NG + 2)
                carry_wait(dve)
                pipeline(dve, l, msg_ahead, msg_cycle, msg_end, msg_front, settle=settled(dve, M, visits_b),
                         steps=[lambda j: update_step(l, j)])
            dve.wait_ge(agg_zeroed, (LAYERS - 1) * NG + 2)
            pipeline(dve, LAYERS - 1, msg_ahead, msg_cycle, msg_end, msg_front, settle=settled(dve, M, visits_b),
                     steps=[norm_step, lambda j: rel_step(0, j, 0, False), lambda j: rel_step(0, j, 1, False)])

            def rel_ahead(n, m, q, c, win):
                build_first(R, c, n, q)

            def rel_cycle(n, m, q, c, win):
                rest = pre[q][:, :].rearrange("p (u d) -> p u d", d=D)
                w0, w1 = win[0]
                dve.wait_ge(R["hi_done"], n + 1)
                dve.wait_ge(R["lo_done"], n + 1)
                nc.vector.tensor_tensor(rest, gath[:, ds((c % BUFFERS) * TILES, TILES), :], m3[q][:, :, 0:D],
                                        ALU.subtract).then_inc(R["rest_done"], 1)
                if -1 in win:
                    add_first(R, visits_r, n - 1, 1 - q, win[-1][0])
                dve.wait_ge(R["mid_done"], n + 1)
                nc.vector.tensor_tensor(m3[q][:, :, 2 * D:], rest, m3[q][:, :, D:2 * D],
                                        ALU.subtract).then_inc(R["lo_done"], 1)
                add_extra(R, visits_r, c, n, q, w0, w1)

            def rel_end(n, m, q, c, win):
                add_first(R, visits_r, n, q, win[0][0])

            for r in range(RLAYERS - 1):
                dve.wait_ge(self_added, 2 * NG * (r + 1))
                pipeline(dve, r, rel_ahead, rel_cycle, rel_end, settle=settled(dve, R, visits_r),
                         steps=[lambda j: rel_step(r + 1, j, 0, True), lambda j: rel_step(r + 1, j, 1, False)])
            dve.wait_ge(self_added, 2 * NG * RLAYERS)
            pipeline(dve, RLAYERS - 1, rel_ahead, rel_cycle, rel_end, settle=settled(dve, R, visits_r),
                     steps=[last_step])


def layouts(x, src, dst, edge_attr_16, edge_type_8, **rest):
    import numpy as np
    n, e = x.shape[0], len(src)
    rows = -(-n // (P * GROUP)) * (P * GROUP)
    if rows == n:
        rows += P * GROUP
    edges = -(-e // (BUFFERS * CHUNK)) * (BUFFERS * CHUNK)

    def fill(a, length, value):
        to = np.full((length, *a.shape[1:]), value, a.dtype)
        to[:len(a)] = a
        return to

    xp = fill(np.asarray(x), rows, 0)
    s, d, t = (fill(np.asarray(a), edges, v) for a, v in ((src, 0), (dst, n), (edge_type_8, 0)))
    attr = fill(np.asarray(edge_attr_16), edges, 0)
    cols = [np.ascontiguousarray(a.reshape(-1, P).T) for a in (s, d, t)]
    arrays = {"xT": np.ascontiguousarray(xp.T), "x_rows": xp, "src": cols[0], "dst": cols[1], "etype": cols[2],
              "dst_rows": d.reshape(-1, CHUNK),
              "edge_attr": np.ascontiguousarray(attr.reshape(-1, TILES, P, attr.shape[1]).transpose(0, 1, 3, 2)
                                           .reshape(edges // CHUNK, -1, P))}
    for k in ("msg_w", "msg_b", "upd_w", "upd_b"):
        arrays[k] = np.ascontiguousarray(rest["L0_gnn_" + k])
    for r in "12":
        for k in ("bases", "coef", "wself", "bias"):
            arrays[k + r] = np.ascontiguousarray(rest["L1_gnn_" + k + r])
    return arrays


def kernel(**inputs):
    import numpy as np
    import concourse.bacc as bacc
    from concourse.bass_utils import run_bass_kernel_spmd

    arrays = layouts(**inputs)
    nc = bacc.Bacc("TRN2", target_bir_lowering=False, num_devices=1)
    args = [nc.dram_tensor("in_" + k, a.shape, mybir.dt.from_np(a.dtype), kind="ExternalInput").ap()
            for k, a in arrays.items()]
    out = nc.dram_tensor("out", list(arrays["x_rows"].shape), F32, kind="ExternalOutput").ap()
    gnn_kernel(nc, *args, out)
    r = run_bass_kernel_spmd(nc, [{"in_" + k: a for k, a in arrays.items()}], core_ids=[0])
    return r.results[0]["out"][:len(inputs["x"])]
```

```python
import concourse.bass as bass
from concourse import mybir
from contextlib import ExitStack

F32 = mybir.dt.float32
BF16 = mybir.dt.bfloat16
I32 = mybir.dt.int32
ALU = mybir.AluOpType
ACT = mybir.ActivationFunctionType
AX = mybir.AxisListType

P = 128
D = 64
TILES = 8
CHUNK = P * TILES
BUFFERS = 4
GROUP = 7
SPLIT = 4
EPS = 1e-5


def gnn_kernel(nc, xT, x_rows, src, dst, etype, dst_rows, edge_attr,
               msg_w, msg_b, upd_w, upd_b,
               bases1, coef1, wself1, bias1, bases2, coef2, wself2, bias2, out, edges):
    NP = xT.shape[1]
    NW = NP // P
    NG = NW // GROUP
    NCH = edge_attr.shape[0]
    NE = edge_attr.shape[1] // TILES
    LAYERS = msg_w.shape[0]
    RLAYERS = 2
    NB, NR = coef1.shape[1], coef1.shape[0]
    PAIRS = NCH // 2
    QUADS = NCH // BUFFERS
    GN = GROUP * P
    LAST = [min(max(-(-edges // P) - (NCH - BUFFERS + b) * TILES, 1), TILES) for b in range(BUFFERS)]
    GATHERS = [(QUADS - 1) * TILES + n for n in LAST]
    assert QUADS > 1
    SEG = PAIRS // NG
    assert SEG > 3
    READY_STEPS = 5 + NG
    HALF = [(0, SPLIT), (SPLIT, GROUP)]
    NORM_STEPS = 13
    LATE = 3 + LAYERS + 4 * RLAYERS
    LOADED = 16 * 3
    FIRST_LOADED = 16 * (1 + 3 * LAYERS)
    ds = bass.ds

    with ExitStack() as ctx:
        def sb(name, shape, dt):
            return ctx.enter_context(nc.sbuf_tensor(name, shape, dt))

        def pb(name, shape, dt=F32):
            return ctx.enter_context(nc.psum_tensor(name, shape, dt))

        def sem(name):
            return ctx.enter_context(nc.semaphore(name))

        msg_table = [nc.dram_tensor(f"msg_table{h}", [NP, D], F32).ap() for h in range(2)]
        rel_table = [nc.dram_tensor(f"rel_table{h}", [NP * NR, D], F32).ap() for h in range(2)]
        range_dram = nc.dram_tensor("range_dram", [NCH, 2], I32).ap()
        base_dram = nc.dram_tensor("base_dram", [NCH], F32).ap()

        src_sb = sb("src_sb", [P, NCH * TILES], I32)
        rel_sb = sb("rel_sb", [P, NCH * TILES], I32)
        dst_sb = sb("dst_sb", [P, NCH * TILES], I32)
        dst_rel = sb("dst_rel", [P, NCH * TILES], F32)
        base_bc = sb("base_bc", [P, NCH], F32)
        extreme = sb("extreme", [PAIRS, 2, 2], I32)
        window_range = sb("window_range", [PAIRS, 2, 2], I32)
        window_base = sb("window_base", [PAIRS, 2], F32)
        range_row = sb("range_row", [1, 2 * NCH], I32)
        ready_row = sb("ready_row", [1, NG], I32)
        first_left = sb("first_left", [1, 1], I32)
        ready_min = sb("ready_min", [1, NG], I32)
        left_at = sb("left_at", [1, NG], I32)
        group_id = sb("group_id", [1, NG], I32)
        group_end = sb("group_end", [1, NG], I32)
        window_start = sb("window_start", [P, NW], F32)
        x_relA = sb("x_relA", [P, TILES], F32)
        x_relB = sb("x_relB", [P, TILES], F32)
        col_id = sb("col_id", [P, P], I32)
        start_id = sb("start_id", [P, NW], I32)
        ident_f = sb("ident_f", [P, P], F32)
        ident_b = sb("ident_b", [P, P], BF16)
        eps_col = sb("eps_col", [P, 1], F32)

        xaT = sb("xaT", [P, NP], F32)
        a3 = sb("a3", [P, NW, 3 * D], BF16)
        b_rows = sb("b_rows", [P, NW, D], F32)
        agg = sb("agg", [P, NW, D], F32)
        xres = sb("xres", [P, NW, D], F32)

        w_ij_all = sb("w_ij_all", [D + 1, LAYERS, 2 * D], F32)
        w_e_diag = sb("w_e_diag", [TILES * NE, LAYERS, TILES * D], F32)
        w_upd_all = sb("w_upd_all", [P, LAYERS, D], F32)
        b_upd_all = sb("b_upd_all", [D, LAYERS], F32)
        w_ij = sb("w_ij", [D + 1, 2 * D], F32)
        w_upd = sb("w_upd", [P, D], F32)
        b_upd = sb("b_upd", [D, 1], F32)
        bases = sb("bases", [D, RLAYERS, NB, D], F32)
        coef = sb("coef", [D, RLAYERS, NR, NB], F32)
        w_rel = sb("w_rel", [D, RLAYERS, NR * D + D], F32)
        w_tmp = sb("w_tmp", [D, NR, D], F32)
        bias_bc = sb("bias_bc", [P, RLAYERS, D], F32)

        idx = [sb(f"idx{b}", [P, TILES], I32) for b in range(BUFFERS)]
        attr = [sb(f"attr{q}", [TILES * NE, P], F32) for q in range(2)]
        gath = sb("gath", [P, BUFFERS * TILES, D], F32)
        hot = [sb(f"hot{q}", [P, TILES, P], BF16) for q in range(2)]
        hotT = sb("hotT", [P, TILES, P], BF16)
        x_hotA = sb("x_hotA", [P, TILES, P], BF16)
        x_hotT = sb("x_hotT", [P, TILES, P], BF16)
        x_hotB = sb("x_hotB", [P, TILES, P], BF16)
        m3 = [sb(f"m3_{q}", [P, TILES, 3 * D], BF16) for q in range(2)]
        part = sb("part", [P, D], F32)
        x_part = sb("x_part", [P, D], F32)

        stage_T = sb("stage_T", [D + 1, GN], F32)
        stage_rows = sb("stage_rows", [P, GROUP, D], F32)
        a_rest = sb("a_rest", [P, GROUP, D], F32)
        rel_buffer = sb("rel_buffer", [P, GROUP, NR * D], F32)
        rel_rows = [rel_buffer[:, k, :] for k in range(GROUP)]
        chunk_dst = rel_buffer[0:PAIRS, :, :].rearrange("p k d -> p (k d)")[:, 0:2 * CHUNK].bitcast(I32) \
            .rearrange("p (a e) -> p a e", a=2)
        zeros = sb("zeros", [P, GROUP, D], F32)
        squares = sb("squares", [P, GROUP, D], F32)
        mean = sb("mean", [P, GROUP], F32)
        var = sb("var", [P, GROUP], F32)
        rstd = sb("rstd", [P, GROUP], F32)
        newton = sb("newton", [P, GROUP], F32)

        hotT_ps = pb("hotT_ps", [P, TILES, P], BF16)
        x_hotT_ps = pb("x_hotT_ps", [P, TILES, P], BF16)
        pre = [pb(f"pre{q}", [P, TILES * D]) for q in range(2)]
        sums = [pb(f"sums{q}", [P, TILES * D]) for q in range(2)]
        x_sums = pb("x_sums", [P, TILES * D])
        col_ps = pb("col_ps", [P, P])
        T_ps = [pre[0][:, :], hotT_ps[:, :, :].rearrange("p a b -> p (a b)").bitcast(F32)]
        upd_ps = [sums[1][:, :], x_hotT_ps[:, :, :].rearrange("p a b -> p (a b)").bitcast(F32)]
        rows_ps = x_sums[:, 0:GROUP * D].rearrange("p (w d) -> p w d", d=D)
        ab_ps = [(x_sums, pre[0])[s][:, 0:(b - a) * 2 * D].rearrange("p (w d) -> p w d", d=2 * D)
                 for s, (a, b) in enumerate(HALF)]
        rel_ps = [T_ps[0], T_ps[1], upd_ps[0]]

        loaded = sem("loaded")
        late_loaded = sem("late_loaded")
        diag_loaded = sem("diag_loaded")
        range_made = sem("range_made")
        range_stored = sem("range_stored")
        range_loaded = sem("range_loaded")
        const_pool = sem("const_pool")
        setup_dve = sem("setup_dve")

        def chunk_sems(k):
            names = ["hot_built", "rows_ready", "z_done", "hi_done", "rest_done", "mid_done", "lo_done", "sums_done",
                     "part_done", "agg_added", "hotT_done", "hotT_copied", "pre_done",
                     "xa_rel", "xa_built", "xa_T", "xa_copied", "xb_rel", "xb_built", "xb_sums", "xb_part", "xb_added"]
            s = {n: sem(f"{k}_{n}") for n in names}
            s["attr_loaded"] = [sem(f"{k}_attr_loaded{q}") for q in range(2)]
            for n in ["idx_loaded", "gathered"]:
                s[n] = [sem(f"{k}_{n}{b}") for b in range(BUFFERS)]
            return s

        M = chunk_sems("msg")
        R = chunk_sems("rel")
        first_loaded = sem("first_loaded")
        agg_zeroed = sem("agg_zeroed")
        xT_staged = sem("xT_staged")
        ab_done = sem("ab_done")
        b_copied = sem("b_copied")
        a_hi = sem("a_hi")
        a_rested = sem("a_rested")
        a_mid = sem("a_mid")
        a_lo = sem("a_lo")
        x_kept = sem("x_kept")
        msg_stored = sem("msg_stored")
        weights_set = sem("weights_set")
        rel_weights = sem("rel_weights")
        rel_rows_made = sem("rel_rows_made")
        ready_made = sem("ready_made")
        agg_staged = sem("agg_staged")
        aggT_done = sem("aggT_done")
        aggT_copied = sem("aggT_copied")
        upd_done = sem("upd_done")
        x_updated = sem("x_updated")
        x3_rows = sem("x3_rows")
        norm = sem("norm")
        var_done = sem("var_done")
        std_done = sem("std_done")
        h_staged = sem("h_staged")
        hT_done = sem("hT_done")
        hT_copied = sem("hT_copied")
        rel_done = sem("rel_done")
        rel_copied = sem("rel_copied")
        rel_stored = sem("rel_stored")
        self_done = sem("self_done")
        self_added = sem("self_added")
        out_stored = sem("out_stored")
        carried = sem("carried")

        block = ctx.enter_context(nc.Block())

        def pipeline(eng, rnd, ahead, cycle, end=None, front=None, ranges=True, steps=(), settle=None):
            STEPS = len(steps)

            def at(step, i, k, win):
                step(rnd * NCH + 2 * i + k, rnd * PAIRS + i + k // 2, k % 2, 2 * i + k, win)

            def whole(i, k, first=False, last=False):
                c, before, after = 2 * i + k, 0 if first else 1, 0 if last else 1
                w = windows(eng, c - before, 1 + before + after) if ranges else []
                pairs = [tuple(w[2 * x:2 * x + 2]) for x in range(len(w) // 2)]
                if front is not None:
                    at(front, i, k, {})
                if not last:
                    at(ahead, i, k + 1, {x - before - 1: v for x, v in enumerate(pairs)})
                at(cycle, i, k, {x - before: v for x, v in enumerate(pairs)})
                if last and end is not None:
                    at(end, i, k, {x - before: v for x, v in enumerate(pairs)})

            def pair(i):
                whole(i, 1)
                whole(i, 2)

            at(ahead, 0, 0, {0: tuple(windows(eng, 0, 1))} if ranges else {})
            whole(0, 0, first=True)
            if STEPS:
                with eng.Fori(0, STEPS) as i:
                    pair(i)
                with eng.Fori(1, NG) as g:
                    with eng.Fori(g * SEG - SEG + STEPS, g * SEG) as i:
                        pair(i)
                    for x, step in enumerate(steps):
                        i = g * SEG + x
                        pair(i)
                        if step is None:
                            continue
                        with eng.If(flag(eng, ready_row[:, ds(g - 1, 1)], 1) > 0):
                            if settle is not None:
                                settle(rnd * NCH + 2 * i + 1)
                            step(g - 1)
            with eng.Fori((NG - 1) * SEG + STEPS if STEPS else 0, PAIRS - 1) as i:
                pair(i)
            whole(PAIRS - 1, 1, last=True)
            if STEPS:
                if settle is not None:
                    settle(rnd * NCH + NCH - 1)
                with eng.Fori(flag(eng, first_left[:, :], NG - 1), NG) as g:
                    with eng.If(flag(eng, ready_row[:, ds(g, 1)], 1) < 1):
                        for step in filter(None, steps):
                            step(g)

        def flag(eng, of, most):
            return nc.values_load_multi_w_load_instructions(
                of, engines=(eng.engine,), min_val=0, max_val=most,
                skip_runtime_bounds_check_because="the kernel worked it out")[1][0]

        def count_in(eng, name):
            reg = eng.alloc_register(name)
            eng.reg_mov(reg, 0)
            return reg

        def settled(eng, S, visits):
            def settle(n):
                k = eng.snap(visits, min_val=0)
                eng.wait_ge(S["xb_added"], k + 1)
                carry_wait(eng)
                eng.wait_ge(S["agg_added"], n + 3)
                carry_wait(eng)
            return settle

        def carry_wait(eng):
            eng.sem_inc(carried, 1)

        def windows(eng, c, count):
            return nc.values_load_multi_w_load_instructions(
                range_row[0:1, ds(2 * c, 2 * count)], engines=(eng.engine,), min_val=0, max_val=NW - 1,
                skip_runtime_bounds_check_because="the destinations are nodes")[1]

        @block.sync
        def _(sp):
            sp.dma_start(xaT[0:D, :], xT).then_inc(first_loaded, 16)
            for l in range(LAYERS):
                sp.dma_start(w_ij_all[0:D, l, 0:D], msg_w[l, 0:D, :]).then_inc(first_loaded, 16)
                sp.dma_start(w_ij_all[0:D, l, D:], msg_w[l, D:2 * D, :]).then_inc(first_loaded, 16)
                sp.dma_start(w_ij_all[D:D + 1, l, 0:D], msg_b[l:l + 1, :]).then_inc(first_loaded, 16)
            sp.dma_start(chunk_dst[:, :, :], dst_rows.rearrange("(p a) e -> p a e", a=2)).then_inc(loaded, 16)
            sp.dma_start(dst_sb[:, :], dst).then_inc(loaded, 16)
            sp.dma_start(src_sb[:, :], src).then_inc(loaded, 16)
            sp.wait_ge(const_pool, 1)
            for u in range(TILES):
                sp.dma_start(w_e_diag[u * NE:(u + 1) * NE, :, u * D:(u + 1) * D],
                             msg_w[:, 2 * D:2 * D + NE, :].rearrange("l i o -> i l o")).then_inc(diag_loaded, 16)
            late = [(w_upd_all[:, :, :], upd_w.rearrange("l i o -> i l o")),
                    (rel_sb[:, :], etype),
                    (xres[:, :, :], x_rows.rearrange("(w p) d -> p w d", p=P))]
            late += [(b_upd_all[:, l:l + 1], upd_b[l, :].unsqueeze(1)) for l in range(LAYERS)]
            for r, (ba, co, ws, bi) in enumerate([(bases1, coef1, wself1, bias1),
                                                  (bases2, coef2, wself2, bias2)]):
                late += [(bases[:, r, :, :], ba.rearrange("b i o -> i b o")),
                         (coef[:, r, :, :], co.unsqueeze(0).to_broadcast([D, NR, NB])),
                         (w_rel[:, r, NR * D:], ws),
                         (bias_bc[:, r, :], bi.unsqueeze(0).to_broadcast([P, D]))]
            assert len(late) == LATE
            for to, of in late:
                sp.dma_start(to, of).then_inc(late_loaded, 16)

            def load_indices(S, c, b, rows):
                sp.dma_start(idx[b][:, :], rows[:, ds(c * TILES, TILES)]).then_inc(S["idx_loaded"][b], 16)

            def load_attributes(c, n, q):
                sp.wait_ge(M["pre_done"], n + 1)
                sp.dma_start(attr[q][:, :], edge_attr[ds(c, 1), :, :].rearrange("a f e -> (a f) e")
                             ).then_inc(M["attr_loaded"][q], 16)

            def chunks(S, rnd, rows, following):
                def gathered(i, b, tiles=TILES):
                    sp.wait_ge(S["gathered"][b], 16 * (rnd * GATHERS[b] + TILES * i + tiles))
                    sp.sem_inc(S["rows_ready"], 1)

                with sp.Fori(0, QUADS - 1) as i:
                    for b in range(BUFFERS):
                        c = BUFFERS * i + b
                        gathered(i, b)
                        load_indices(S, c + BUFFERS, b, rows)
                        if S is M:
                            load_attributes(c + 2, rnd * NCH + c + 2, b % 2)
                for b in range(BUFFERS):
                    c = NCH - BUFFERS + b
                    gathered(QUADS - 1, b, LAST[b])
                    if following is not None:
                        load_indices(following[0], b, b, following[1])
                    if S is M and c + 2 < NCH:
                        load_attributes(c + 2, rnd * NCH + c + 2, b % 2)
                    elif S is M and following[0] is M:
                        load_attributes(c + 2 - NCH, rnd * NCH + c + 2, b % 2)

            sp.wait_ge(loaded, LOADED)
            for b in range(BUFFERS):
                load_indices(M, b, b, src_sb)
            for q in range(2):
                load_attributes(q, q, q)
            sp.wait_ge(range_made, 4)
            sp.dma_start(range_dram.rearrange("(p a) b -> p (a b)", a=2),
                         window_range[:, :, :].rearrange("p a b -> p (a b)")).then_inc(range_stored, 16)
            sp.dma_start(base_dram.rearrange("(p a) -> p a", a=2), window_base[:, :]).then_inc(range_stored, 16)
            sp.wait_ge(range_stored, 32)
            sp.dma_start(range_row[:, :], range_dram.rearrange("(o c) b -> o (c b)", o=1)).then_inc(range_loaded, 16)
            sp.dma_start(base_bc[:, :], base_dram.unsqueeze(0).to_broadcast([P, NCH])).then_inc(range_loaded, 16)
            with sp.Fori(0, LAYERS - 1) as l:
                chunks(M, l, src_sb, (M, src_sb))
            sp.wait_ge(rel_rows_made, 1)
            chunks(M, LAYERS - 1, src_sb, (R, rel_sb))
            with sp.Fori(0, RLAYERS - 1) as r:
                chunks(R, r, rel_sb, (R, rel_sb))
            chunks(R, RLAYERS - 1, rel_sb, None)
            sp.wait_ge(out_stored, 16 * NG)

        @block.gpsimd
        def _(pool):
            pool.memset(w_e_diag[:, :, :], 0.0).then_inc(const_pool, 1)
            pool.iota(col_id[:, :], [[1, P]], base=0, channel_multiplier=0).then_inc(const_pool, 1)
            pool.memset(ident_f[:, :], 0.0).then_inc(const_pool, 1)
            pool.memset(eps_col[:, :], EPS).then_inc(const_pool, 1)
            pool.wait_ge(const_pool, 4)
            pool.affine_select(ident_f[:, :], ident_f[:, :], [[-1, P]], ALU.not_equal, 1.0, base=0,
                               channel_multiplier=1).then_inc(const_pool, 1)
            pool.iota(start_id[:, :], [[P, NW]], base=0, channel_multiplier=0).then_inc(const_pool, 1)
            pool.iota(group_end[:, :], [[GROUP, NG]], base=GROUP, channel_multiplier=0).then_inc(const_pool, 1)
            pool.iota(group_id[:, :], [[1, NG]], base=0, channel_multiplier=0).then_inc(const_pool, 1)

            def gather(S, table, rnd, i, b, used, tiles=TILES):
                pool.wait_ge(S["idx_loaded"][b], 16 * (rnd * QUADS + i + 1))
                pool.wait_ge(S[used], rnd * NCH + BUFFERS * i + b + 1)
                carry_wait(pool)
                for u in range(tiles):
                    pool.indirect_dma_start(gath[:, b * TILES + u, :], None, table,
                                            bass.IndirectOffsetOnAxis(ap=idx[b][:, u:u + 1], axis=0)
                                            ).then_inc(S["gathered"][b], 16)

            for l in range(LAYERS):
                pool.wait_ge(msg_stored, 16 * NG * (l + 1))
                with pool.Fori(0, QUADS - 1) as i:
                    for b in range(BUFFERS):
                        gather(M, msg_table[l % 2], l, i, b, "z_done")
                for b in range(BUFFERS):
                    gather(M, msg_table[l % 2], l, QUADS - 1, b, "z_done", LAST[b])
            for r in range(RLAYERS):
                pool.wait_ge(rel_stored, 16 * NW * (r + 1))
                with pool.Fori(0, QUADS - 1) as i:
                    for b in range(BUFFERS):
                        gather(R, rel_table[r % 2], r, i, b, "rest_done")
                for b in range(BUFFERS):
                    gather(R, rel_table[r % 2], r, QUADS - 1, b, "rest_done", LAST[b])

        @block.scalar
        def _(act):
            visits = act.alloc_register("act_visits")
            act.reg_mov(visits, 0)
            act.sem_inc(M["hotT_copied"], 1)
            act.sem_inc(b_copied, 2)
            updates, norms, rels = (count_in(act, "act_" + name) for name in ("updates", "norms", "rels"))

            def msg_ahead(n, m, q, c, win):
                w0, w1 = win[0]
                act.wait_ge(M["hotT_done"], n + 1)
                act.activation(hotT[:, :, :], hotT_ps[:, :, :], ACT.Copy).then_inc(M["hotT_copied"], 1)
                with act.If(w0 < w1):
                    with act.Fori(w0, w1):
                        k = act.snap(visits, min_val=0)
                        act.wait_ge(M["xa_T"], k + 2)
                        act.activation(x_hotT[:, :, :], x_hotT_ps[:, :, :], ACT.Copy).then_inc(M["xa_copied"], 1)
                        act.reg_add(visits, visits, 1)

            def msg_front(n, m, q, c, win):
                z = pre[q][:, :].rearrange("p (u d) -> p u d", d=D)
                act.wait_ge(M["z_done"], n + BUFFERS + 1)
                act.wait_ge(M["sums_done"], n + 1)
                act.activation(m3[q][:, :, 0:D], z, ACT.Relu).then_inc(M["hi_done"], 1)

            def msg_cycle(n, m, q, c, win):
                z = pre[q][:, :].rearrange("p (u d) -> p u d", d=D)
                act.wait_ge(M["rest_done"], n + 1)
                act.activation(m3[q][:, :, D:2 * D], z, ACT.Copy).then_inc(M["mid_done"], 1)

            def msg_tables(l, t, j):
                w0 = j * GROUP

                def store(h):
                    act.dma_start(msg_table[h][ds(j * GN, GN), :].rearrange("(w p) d -> p w d", p=P),
                                  b_rows[:, ds(j * GROUP, GROUP), :]).then_inc(msg_stored, 16)

                for s, (a, b) in enumerate(HALF):
                    act.wait_ge(ab_done, 2 * t + s + 1)
                    act.activation(b_rows[:, ds(w0 + a, b - a), :], ab_ps[s][:, :, D:], ACT.Copy).then_inc(b_copied, 1)
                    act.activation(a3[:, ds(w0 + a, b - a), 0:D], ab_ps[s][:, :, 0:D], ACT.Copy).then_inc(a_hi, 1)
                act.wait_ge(b_copied, 2 * t + 4)
                if l is None:
                    store(0)
                else:
                    for h in range(2):
                        with act.If(l % 2 < 1 if h == 0 else l % 2 > 0):
                            store(h)
                act.wait_ge(a_rested, 2 * t + 4)
                act.activation(a3[:, ds(j * GROUP, GROUP), D:2 * D], a_rest[:, :, :], ACT.Copy).then_inc(a_mid, 1)

            def update(t, j):
                for s, (a, b) in enumerate(HALF):
                    act.wait_ge(aggT_done, 2 * t + s + 1)
                    act.activation(xaT[D:2 * D, ds(j * GN + a * P, (b - a) * P)],
                                   T_ps[s][0:D, 0:(b - a) * P], ACT.Copy).then_inc(aggT_copied, 1)
                for s, (a, b) in enumerate(HALF):
                    act.wait_ge(upd_done, 2 * t + s + 1)
                    act.activation(stage_T[0:D, a * P:b * P], upd_ps[s][0:D, 0:(b - a) * P],
                                   ACT.Relu, bias=b_upd[:, :]).then_inc(x_updated, 1)

            def root(t):
                act.wait_ge(var_done, t + 1)
                act.activation(rstd[:, :], var[:, :], ACT.Sqrt, bias=eps_col[:, :]).then_inc(std_done, 1)

            with act.Fori(0, NG) as j:
                msg_tables(None, j, j)
            act.wait_ge(first_loaded, FIRST_LOADED)
            act.wait_ge(late_loaded, 16 * LATE)
            act.wait_ge(ready_made, READY_STEPS)

            def set_weights(l):
                act.wait_ge(ab_done, 2 * (l + 1) * NG)
                act.activation(w_upd[:, :], w_upd_all[:, ds(l, 1), :].rearrange("p a d -> p (a d)"),
                               ACT.Copy).then_inc(weights_set, 1)
                act.activation(b_upd[:, :], b_upd_all[:, ds(l, 1)], ACT.Copy).then_inc(weights_set, 1)

            def update_step(l, j):
                t = act.snap(updates, min_val=0)
                update(t, j)
                msg_tables(l + 1, t + NG, j)
                act.reg_add(updates, updates, 1)

            def norm_step(j):
                t = act.snap(norms, min_val=0)
                update(t + (LAYERS - 1) * NG, j)
                root(t)
                act.reg_add(norms, norms, 1)

            def rel_step(r, j, s):
                t = act.snap(rels, min_val=0)
                if s == 0:
                    for x, (a, b) in enumerate(HALF):
                        act.wait_ge(hT_done, 2 * t + x + 1)
                        act.activation(stage_T[0:D, a * P:b * P], T_ps[x][0:D, 0:(b - a) * P],
                                       ACT.Copy).then_inc(hT_copied, 1)
                    with act.If(t > 0):
                        act.wait_ge(rel_stored, t * GROUP * 16)
                        carry_wait(act)
                for k in range(*HALF[s]):
                    act.wait_ge(rel_done, t * GROUP + k + 1)
                    act.activation(rel_rows[k], rel_ps[k % 3], ACT.Copy).then_inc(rel_copied, 1)
                    act.wait_ge(rel_copied, t * GROUP + k + 1)
                    act.dma_start(rel_table[r % 2][ds((j * GROUP + k) * (P * NR), P * NR), :]
                                  .rearrange("(p a) d -> p (a d)", a=NR), rel_rows[k]).then_inc(rel_stored, 16)
                if s == 1:
                    act.reg_add(rels, rels, 1)

            with act.Fori(0, LAYERS - 1) as l:
                set_weights(l)
                act.activation(w_ij[:, :], w_ij_all[:, ds(l + 1, 1), :].rearrange("p a d -> p (a d)"),
                               ACT.Copy).then_inc(weights_set, 1)
                pipeline(act, l, msg_ahead, msg_cycle, front=msg_front, steps=[lambda j: update_step(l, j)])
            set_weights(LAYERS - 1)
            pipeline(act, LAYERS - 1, msg_ahead, msg_cycle, front=msg_front,
                     steps=[norm_step, lambda j: rel_step(0, j, 0), lambda j: rel_step(0, j, 1)])

            def rel_ahead(n, m, q, c, win):
                pass

            def rel_cycle(n, m, q, c, win):
                act.wait_ge(R["rows_ready"], n + 1)
                act.wait_ge(R["sums_done"], n + 1)
                act.activation(m3[q][:, :, 0:D], gath[:, ds((c % BUFFERS) * TILES, TILES), :],
                               ACT.Copy).then_inc(R["hi_done"], 1)
                act.wait_ge(R["rest_done"], n + BUFFERS + 1)
                act.activation(m3[q][:, :, D:2 * D], pre[q][:, :].rearrange("p (u d) -> p u d", d=D),
                               ACT.Copy).then_inc(R["mid_done"], 1)

            def last_step(j):
                t = act.snap(norms, min_val=0)
                root(t)
                act.wait_ge(norm, NORM_STEPS * (t + 1))
                act.dma_start(out[ds(j * GN, GN), :].rearrange("(w p) d -> p w d", p=P),
                              xres[:, ds(j * GROUP, GROUP), :]).then_inc(out_stored, 16)
                act.reg_add(norms, norms, 1)

            for r in range(RLAYERS - 1):
                pipeline(act, r, rel_ahead, rel_cycle, ranges=False,
                         steps=[lambda j: rel_step(r + 1, j, 0), lambda j: rel_step(r + 1, j, 1)])
            pipeline(act, RLAYERS - 1, rel_ahead, rel_cycle, ranges=False, steps=[last_step])

        @block.tensor
        def _(pe):
            visits_a = pe.alloc_register("pe_visits_a")
            visits_b = pe.alloc_register("pe_visits_b")
            visits_r = pe.alloc_register("pe_visits_r")
            for reg in (visits_a, visits_b, visits_r):
                pe.reg_mov(reg, 0)
            pe.sem_inc(M["sums_done"], 2)
            pe.sem_inc(R["sums_done"], 2)
            pe.sem_inc(M["pre_done"], 2)
            pe.sem_inc(M["xa_T"], 1)
            updates, norms, rels = (count_in(pe, "pe_" + name) for name in ("updates", "norms", "rels"))

            def transposes(to, of):
                for u in range(TILES):
                    last = nc.tensor.transpose(to[:, u, :], of[:, u, :], ident_b[:, :])
                return last

            def expand(to, of, w, stop):
                for u in range(TILES):
                    for k in range(3):
                        last = nc.tensor.matmul(to[:, u * D:(u + 1) * D], of[:, u, :],
                                                a3[:, ds(w, 1), k * D:(k + 1) * D].rearrange("p a d -> p (a d)"),
                                                start=False, stop=stop and k == 2 and u == TILES - 1)
                return last

            def sum_up(to, hots, parts):
                for u in range(TILES):
                    last = nc.tensor.matmul(to[:, 0:3 * D], hots[:, u, :], parts[:, u, :],
                                            start=u == 0, stop=u == TILES - 1)
                return last

            def msg_ahead(l, n, m, q, c, win):
                w0, w1 = win[0]
                pe.wait_ge(M["attr_loaded"][q], 16 * (m + 1))
                pe.wait_ge(M["lo_done"], n + 1)
                nc.tensor.matmul(pre[q][:, :], attr[q][:, :],
                                 w_e_diag[:, ds(l, 1), :].rearrange("p a d -> p (a d)"), start=True, stop=False)
                pe.wait_ge(M["hot_built"], n + 1)
                pe.wait_ge(M["hotT_copied"], n + 1)
                transposes(hotT_ps, hot[q]).then_inc(M["hotT_done"], 1)
                with pe.If(w0 < w1):
                    with pe.Fori(w0, w1) as w:
                        k = pe.snap(visits_a, min_val=0)
                        pe.wait_ge(M["xa_built"], k + 1)
                        transposes(x_hotT_ps, x_hotA).then_inc(M["xa_T"], 1)
                        pe.wait_ge(M["xa_copied"], k + 1)
                        expand(pre[q], x_hotT, w + 1, False)
                        pe.reg_add(visits_a, visits_a, 1)
                pe.wait_ge(M["hotT_copied"], n + 2)
                expand(pre[q], hotT, w0, True).then_inc(M["pre_done"], 1)

            def sums_cycle(S, visits):
                def run(n, m, q, c, win):
                    w0, w1 = win[0]
                    with pe.If(w0 < w1):
                        with pe.Fori(w0, w1):
                            k = pe.snap(visits, min_val=0)
                            pe.wait_ge(S["xb_built"], k + 1)
                            sum_up(x_sums, x_hotB, m3[q]).then_inc(S["xb_sums"], 1)
                            pe.reg_add(visits, visits, 1)
                    pe.wait_ge(S["agg_added"], n + 1)
                    pe.wait_ge(S["lo_done"], n + 3)
                    sum_up(sums[q], hot[q], m3[q]).then_inc(S["sums_done"], 1)
                return run

            def rel_ahead(n, m, q, c, win):
                pe.wait_ge(R["hot_built"], n + 1)
                carry_wait(pe)

            def msg_tables(t, weights, staged=None):
                for s, (a, b) in enumerate(HALF):
                    if staged is not None:
                        pe.wait_ge(staged, 2 * t + s + 1)
                    pe.wait_ge(b_copied, 2 * t + s + 1)
                    pe.wait_ge(a_rested, 2 * t + s + 1)
                    carry_wait(pe)
                    for w in range(a, b):
                        last = nc.tensor.matmul(ab_ps[s][:, w - a, :], stage_T[:, w * P:(w + 1) * P], weights,
                                                start=True, stop=True)
                    last.then_inc(ab_done, 1)

            def transpose_rows(done):
                for s, (a, b) in enumerate(HALF):
                    for w in range(a, b):
                        last = nc.tensor.transpose(T_ps[s][0:D, (w - a) * P:(w - a + 1) * P],
                                                   stage_rows[:, w, :], ident_f[:, :])
                    last.then_inc(done, 1)

            def update(t, j):
                pe.wait_ge(agg_staged, t + 1)
                carry_wait(pe)
                transpose_rows(aggT_done)
                for s, (a, b) in enumerate(HALF):
                    pe.wait_ge(aggT_copied, 2 * t + s + 1)
                    nc.tensor.matmul(upd_ps[s][0:D, 0:(b - a) * P], w_upd[:, :],
                                     xaT[:, ds(j * GN + a * P, (b - a) * P)],
                                     start=True, stop=True).then_inc(upd_done, 1)
                pe.wait_ge(x_updated, 2 * t + 2)

            def update_step(l, j):
                t = pe.snap(updates, min_val=0)
                update(t, j)
                msg_tables(t + NG, w_ij[:, :])
                pe.wait_ge(b_copied, 2 * (t + NG) + 4)
                pe.wait_ge(a_lo, t + NG + 2)
                pe.wait_ge(x_kept, t + 1)
                carry_wait(pe)
                pe.reg_add(updates, updates, 1)

            def norm_step(j):
                t = pe.snap(norms, min_val=0)
                update(t + (LAYERS - 1) * NG, j)
                carry_wait(pe)
                for w in range(GROUP):
                    last = nc.tensor.transpose(x_sums[:, w * D:(w + 1) * D], stage_T[0:D, w * P:(w + 1) * P],
                                               ident_f[0:D, 0:D])
                last.then_inc(x3_rows, 1)
                pe.wait_ge(norm, NORM_STEPS * t + 1)
                carry_wait(pe)
                pe.reg_add(norms, norms, 1)

            def rel_step(r, j, s):
                t = pe.snap(rels, min_val=0)
                if s == 0:
                    pe.wait_ge(h_staged, t + 1)
                    carry_wait(pe)
                    transpose_rows(hT_done)
                    pe.wait_ge(hT_copied, 2 * t + 2)
                    carry_wait(pe)
                a, b = HALF[s]
                for k in range(a, b):
                    if k >= a + 3:
                        pe.wait_ge(rel_copied, t * GROUP + k - 2)
                        carry_wait(pe)
                    nc.tensor.matmul(rel_ps[k % 3], stage_T[0:D, k * P:(k + 1) * P],
                                     w_rel[:, ds(r, 1), 0:NR * D].rearrange("p a d -> p (a d)"),
                                     start=True, stop=True).then_inc(rel_done, 1)
                if s == 1:
                    for k in range(GROUP):
                        last = nc.tensor.matmul(x_sums[:, k * D:(k + 1) * D], stage_T[0:D, k * P:(k + 1) * P],
                                                w_rel[:, ds(r, 1), NR * D:].rearrange("p a d -> p (a d)"),
                                                start=True, stop=True)
                    last.then_inc(self_done, 1)
                pe.wait_ge(rel_copied, t * GROUP + b)
                carry_wait(pe)
                if s == 1:
                    pe.wait_ge(self_added, t + 1)
                    carry_wait(pe)
                    pe.reg_add(rels, rels, 1)

            pe.wait_ge(setup_dve, 1)
            pe.wait_ge(const_pool, 8)
            with pe.Fori(0, NG) as j:
                msg_tables(j, w_ij_all[:, 0, :], staged=xT_staged)
            pe.wait_ge(b_copied, 2 * NG + 2)
            pe.wait_ge(a_lo, NG + 1)
            with pe.Fori(0, LAYERS - 1) as l:
                pe.wait_ge(weights_set, 3 * (l + 1))
                carry_wait(pe)
                pe.wait_ge(ready_made, READY_STEPS)
                pe.wait_ge(diag_loaded, 16 * TILES)
                pipeline(pe, l, lambda *at: msg_ahead(l, *at), sums_cycle(M, visits_b),
                         settle=settled(pe, M, visits_b), steps=[lambda j: update_step(l, j)])
            pe.wait_ge(weights_set, 3 * LAYERS - 1)
            pipeline(pe, LAYERS - 1, lambda *at: msg_ahead(LAYERS - 1, *at), sums_cycle(M, visits_b),
                     settle=settled(pe, M, visits_b),
                     steps=[norm_step, lambda j: rel_step(0, j, 0), lambda j: rel_step(0, j, 1)])
            for r in range(RLAYERS - 1):
                pipeline(pe, r, rel_ahead, sums_cycle(R, visits_r), settle=settled(pe, R, visits_r),
                         steps=[lambda j: rel_step(r + 1, j, 0), lambda j: rel_step(r + 1, j, 1)])
            pipeline(pe, RLAYERS - 1, rel_ahead, sums_cycle(R, visits_r))

        @block.vector
        def _(dve):
            visits_a = dve.alloc_register("dve_visits_a")
            visits_b = dve.alloc_register("dve_visits_b")
            visits_r = dve.alloc_register("dve_visits_r")
            for reg in (visits_a, visits_b, visits_r):
                dve.reg_mov(reg, 0)
            for S in (M, R):
                dve.sem_inc(S["lo_done"], 2)
                dve.sem_inc(S["agg_added"], 2)
                dve.sem_inc(S["xb_added"], 1)
            dve.sem_inc(M["z_done"], BUFFERS)
            dve.sem_inc(R["rest_done"], BUFFERS)
            dve.sem_inc(a_lo, 1)
            dve.sem_inc(a_rested, 2)
            updates, norms, rels = (count_in(dve, "dve_" + name) for name in ("updates", "norms", "rels"))

            nc.vector.memset(stage_T[D:D + 1, :], 1.0)
            nc.vector.memset(w_ij_all[D:D + 1, :, D:], 0.0)
            dve.wait_ge(const_pool, 8)
            nc.vector.tensor_copy(col_ps[:, :], col_id[:, :])
            nc.vector.tensor_copy(window_start[:, :], start_id[:, :])
            nc.vector.tensor_copy(ident_b[:, :], ident_f[:, :]).then_inc(setup_dve, 1)
            cols = col_ps[:, :].unsqueeze(1).to_broadcast([P, TILES, P])

            def build_first(S, c, n, q):
                dve.wait_ge(S["sums_done"], n + 1)
                nc.vector.tensor_tensor(hot[q][:, :, :], cols,
                                        dst_rel[:, ds(c * TILES, TILES)].unsqueeze(2).to_broadcast([P, TILES, P]),
                                        ALU.is_equal).then_inc(S["hot_built"], 1)

            def build(to, rel, rel_made, done, k, c, w):
                nc.vector.tensor_tensor(rel[:, :], dst_sb[:, ds(c * TILES, TILES)],
                                        window_start[:, ds(w, 1)].to_broadcast([P, TILES]),
                                        ALU.subtract).then_inc(rel_made, 1)
                dve.wait_ge(rel_made, k + 1)
                nc.vector.tensor_tensor(to[:, :, :], cols, rel[:, :].unsqueeze(2).to_broadcast([P, TILES, P]),
                                        ALU.is_equal).then_inc(done, 1)

            def add_extra(S, visits, c, n, q, w0, w1):
                with dve.If(w0 < w1):
                    with dve.Fori(w0, w1) as w:
                        k = dve.snap(visits, min_val=0)
                        dve.wait_ge(S["xb_added"], k + 1)
                        dve.wait_ge(S["agg_added"], n + 2)
                        build(x_hotB, x_relB, S["xb_rel"], S["xb_built"], k, c, w + 1)
                        dve.wait_ge(S["xb_sums"], k + 1)
                        nc.vector.tensor_reduce(x_part[:, :], x_sums[:, 0:3 * D].rearrange("p (k d) -> p d k", d=D),
                                                AX.X, ALU.add).then_inc(S["xb_part"], 1)
                        dve.wait_ge(S["xb_part"], k + 1)
                        to = agg[:, ds(w + 1, 1), :].rearrange("p a d -> p (a d)")
                        nc.vector.tensor_tensor(to, to, x_part[:, :], ALU.add).then_inc(S["xb_added"], 1)
                        dve.reg_add(visits, visits, 1)

            def add_first(S, visits, n, q, w0):
                k = dve.snap(visits, min_val=0)
                dve.wait_ge(S["xb_added"], k + 1)
                dve.wait_ge(S["agg_added"], n + 2)
                dve.wait_ge(S["sums_done"], n + 3)
                nc.vector.tensor_reduce(part[:, :], sums[q][:, 0:3 * D].rearrange("p (k d) -> p d k", d=D),
                                        AX.X, ALU.add).then_inc(S["part_done"], 1)
                dve.wait_ge(S["part_done"], n + 1)
                to = agg[:, ds(w0, 1), :].rearrange("p a d -> p (a d)")
                nc.vector.tensor_tensor(to, to, part[:, :], ALU.add).then_inc(S["agg_added"], 1)

            def msg_ahead(n, m, q, c, win):
                w0, w1 = win[0]
                build_first(M, c, n, q)
                with dve.If(w0 < w1):
                    with dve.Fori(w0, w1) as w:
                        k = dve.snap(visits_a, min_val=0)
                        dve.wait_ge(M["xa_T"], k + 1)
                        build(x_hotA, x_relA, M["xa_rel"], M["xa_built"], k, c, w + 1)
                        dve.reg_add(visits_a, visits_a, 1)

            def msg_front(n, m, q, c, win):
                z = pre[q][:, :].rearrange("p (u d) -> p u d", d=D)
                dve.wait_ge(M["pre_done"], n + 3)
                dve.wait_ge(M["rows_ready"], n + 1)
                nc.vector.tensor_tensor(z, z, gath[:, ds((c % BUFFERS) * TILES, TILES), :], ALU.add).then_inc(M["z_done"], 1)

            def msg_cycle(n, m, q, c, win):
                z = pre[q][:, :].rearrange("p (u d) -> p u d", d=D)
                w0, w1 = win[0]
                if -1 in win:
                    add_first(M, visits_b, n - 1, 1 - q, win[-1][0])
                dve.wait_ge(M["hi_done"], n + 1)
                nc.vector.scalar_tensor_tensor(z, z, 0.0, m3[q][:, :, 0:D], ALU.max,
                                               ALU.subtract).then_inc(M["rest_done"], 1)
                dve.wait_ge(M["mid_done"], n + 1)
                nc.vector.tensor_tensor(m3[q][:, :, 2 * D:], z, m3[q][:, :, D:2 * D],
                                        ALU.subtract).then_inc(M["lo_done"], 1)
                add_extra(M, visits_b, c, n, q, w0, w1)

            def split_tables(t, j, between=None):
                dve.wait_ge(a_lo, t + 1)
                for s, (a, b) in enumerate(HALF):
                    if between is not None:
                        between(s)
                    dve.wait_ge(a_hi, 2 * t + s + 1)
                    nc.vector.tensor_tensor(a_rest[:, a:b, :], ab_ps[s][:, :, 0:D],
                                            a3[:, ds(j * GROUP + a, b - a), 0:D],
                                            ALU.subtract).then_inc(a_rested, 1)
                dve.wait_ge(a_mid, t + 1)
                to = a3[:, ds(j * GROUP, GROUP), :]
                nc.vector.tensor_tensor(to[:, :, 2 * D:], a_rest[:, :, :], to[:, :, D:2 * D],
                                        ALU.subtract).then_inc(a_lo, 1)

            def msg_end(n, m, q, c, win):
                add_first(M, visits_b, n, q, win[0][0])

            nc.vector.memset(zeros[:, :, :], 0.0).then_inc(agg_zeroed, 1)
            nc.vector.memset(agg[:, :, :], 0.0).then_inc(agg_zeroed, 1)

            def stage_x(j, s):
                a, b = HALF[s]
                if isinstance(j, int):
                    of = xaT[0:D, j * GN + a * P:j * GN + b * P]
                else:
                    of = xaT[0:D, ds(j * GN + a * P, (b - a) * P)]
                nc.vector.tensor_copy(stage_T[0:D, a * P:b * P], of).then_inc(xT_staged, 1)

            def first_tables(j, more):
                def stage_next(s):
                    dve.wait_ge(ab_done, 2 * j + s + 1)
                    stage_x(j + 1, s)

                split_tables(j, j, stage_next if more else None)

            dve.wait_ge(first_loaded, FIRST_LOADED)
            for s in range(2):
                stage_x(0, s)
            with dve.Fori(0, NG - 1) as j:
                first_tables(j, True)
            first_tables(NG - 1, False)
            dve.wait_ge(loaded, LOADED)
            nc.vector.tensor_reduce(extreme[:, :, 0], chunk_dst[:, :, :], AX.X, ALU.min).then_inc(range_made, 1)
            nc.vector.tensor_reduce(extreme[:, :, 1], chunk_dst[:, :, :], AX.X, ALU.max).then_inc(range_made, 1)
            dve.wait_ge(range_made, 2)
            nc.vector.tensor_scalar(window_range[:, :, :], extreme[:, :, :], 7, None,
                                    ALU.arith_shift_right).then_inc(range_made, 1)
            dve.wait_ge(range_made, 3)
            nc.vector.tensor_scalar(window_base[:, :], window_range[:, :, 0], float(P), None,
                                    ALU.mult).then_inc(range_made, 1)
            dve.wait_ge(range_loaded, 32)
            nc.vector.tensor_tensor(dst_rel[:, :].rearrange("p (c u) -> p c u", u=TILES),
                                    dst_sb[:, :].rearrange("p (c u) -> p c u", u=TILES),
                                    base_bc[:, :].unsqueeze(2).to_broadcast([P, NCH, TILES]),
                                    ALU.subtract).then_inc(ready_made, 1)
            nc.vector.memset(ready_min[:, :], 0).then_inc(ready_made, 1)
            dve.wait_ge(ready_made, 2)
            lows = range_row[:, :].rearrange("o (c b) -> o c b", b=2)
            for j in range(NG - 1):
                nc.vector.tensor_reduce(ready_min[:, j:j + 1], lows[:, 2 * ((j + 1) * SEG + 1):, 0], AX.X,
                                        ALU.min).then_inc(ready_made, 1)
            dve.wait_ge(ready_made, 1 + NG)
            nc.vector.tensor_tensor(ready_row[:, :], ready_min[:, :], group_end[:, :],
                                    ALU.is_ge).then_inc(ready_made, 1)
            dve.wait_ge(ready_made, 2 + NG)
            nc.vector.tensor_scalar(left_at[:, :], ready_row[:, :], float(NG), None, ALU.mult).then_inc(ready_made, 1)
            dve.wait_ge(ready_made, 3 + NG)
            nc.vector.tensor_tensor(left_at[:, :], left_at[:, :], group_id[:, :], ALU.add).then_inc(ready_made, 1)
            dve.wait_ge(ready_made, 4 + NG)
            nc.vector.tensor_reduce(first_left[:, :], left_at[:, :], AX.X, ALU.min).then_inc(ready_made, 1)
            dve.wait_ge(ready_made, READY_STEPS)

            dve.wait_ge(late_loaded, 16 * LATE)
            chain = 0
            for r in range(RLAYERS):
                w = w_rel[:, r, 0:NR * D].rearrange("p (r d) -> p r d", d=D)
                for b in range(NB):
                    to = w if b == 0 else w_tmp[:, :, :]
                    nc.vector.tensor_tensor(to, bases[:, r, b, :].unsqueeze(1).to_broadcast([D, NR, D]),
                                            coef[:, r, :, b].unsqueeze(2).to_broadcast([D, NR, D]),
                                            ALU.mult).then_inc(rel_weights, 1)
                    chain += 1
                    dve.wait_ge(rel_weights, chain)
                    if b:
                        nc.vector.tensor_tensor(w, w, w_tmp[:, :, :], ALU.add).then_inc(rel_weights, 1)
                        chain += 1
                        dve.wait_ge(rel_weights, chain)
            nc.vector.scalar_tensor_tensor(rel_sb[:, :], src_sb[:, :], float(NR), rel_sb[:, :],
                                           ALU.mult, ALU.add).then_inc(rel_rows_made, 1)
            def stage_agg(j, done):
                nc.vector.tensor_copy(stage_rows[:, :, :], agg[:, ds(j * GROUP, GROUP), :]).then_inc(done, 1)

            def update_step(l, j):
                t = dve.snap(updates, min_val=0)
                stage_agg(j, agg_staged)
                dve.wait_ge(x_updated, 2 * t + 2)
                nc.vector.tensor_copy(xaT[0:D, ds(j * GN, GN)], stage_T[0:D, :]).then_inc(x_kept, 1)
                nc.vector.tensor_copy(agg[:, ds(j * GROUP, GROUP), :], zeros[:, :, :]).then_inc(agg_zeroed, 1)
                split_tables(t + NG, j)
                dve.reg_add(updates, updates, 1)

            def layer_norm(t, j, more, copy_to):
                at = 0
                bc = [P, GROUP, D]
                x = xres[:, ds(j * GROUP, GROUP), :]

                def step(ins):
                    nonlocal at
                    at += 1
                    ins.then_inc(norm, 1)
                    dve.wait_ge(norm, t * NORM_STEPS + at)
                    carry_wait(dve)

                step(nc.vector.tensor_tensor(x, x, more, ALU.add))
                step(nc.vector.tensor_reduce(mean[:, :], x, AX.X, ALU.add))
                step(nc.vector.tensor_scalar(mean[:, :], mean[:, :], 1.0 / D, None, ALU.mult))
                step(nc.vector.tensor_tensor(x, x, mean[:, :].unsqueeze(2).to_broadcast(bc), ALU.subtract))
                step(nc.vector.tensor_tensor(squares[:, :, :], x, x, ALU.mult))
                step(nc.vector.tensor_reduce(var[:, :], squares[:, :, :], AX.X, ALU.add))
                nc.vector.tensor_scalar(var[:, :], var[:, :], 1.0 / D, None, ALU.mult).then_inc(var_done, 1)
                dve.wait_ge(std_done, t + 1)
                carry_wait(dve)
                step(nc.vector.reciprocal(rstd[:, :], rstd[:, :]))
                step(nc.vector.tensor_tensor(newton[:, :], rstd[:, :], rstd[:, :], ALU.mult))
                step(nc.vector.tensor_scalar(var[:, :], var[:, :], EPS, None, ALU.add))
                step(nc.vector.tensor_tensor(newton[:, :], newton[:, :], var[:, :], ALU.mult))
                step(nc.vector.tensor_scalar(newton[:, :], newton[:, :], -0.5, 1.5, ALU.mult, ALU.add))
                step(nc.vector.tensor_tensor(rstd[:, :], rstd[:, :], newton[:, :], ALU.mult))
                step(nc.vector.tensor_tensor(x, x, rstd[:, :].unsqueeze(2).to_broadcast(bc), ALU.mult))
                if copy_to is not None:
                    nc.vector.tensor_copy(copy_to, x).then_inc(h_staged, 1)
                assert at == NORM_STEPS

            def norm_step(j):
                t = dve.snap(norms, min_val=0)
                stage_agg(j, agg_staged)
                dve.wait_ge(x3_rows, t + 1)
                carry_wait(dve)
                layer_norm(t, j, rows_ps, stage_rows[:, :, :])
                dve.reg_add(norms, norms, 1)

            def stage_step(j):
                stage_agg(j, h_staged)

            def self_step(r, j):
                t = dve.snap(rels, min_val=0)
                dve.wait_ge(self_done, t + 1)
                nc.vector.tensor_tensor(agg[:, ds(j * GROUP, GROUP), :], rows_ps,
                                        bias_bc[:, ds(r, 1), :].to_broadcast([P, GROUP, D]),
                                        ALU.add).then_inc(self_added, 1)
                dve.reg_add(rels, rels, 1)

            def last_step(j):
                t = dve.snap(norms, min_val=0)
                layer_norm(t, j, agg[:, ds(j * GROUP, GROUP), :], None)
                dve.reg_add(norms, norms, 1)

            with dve.Fori(0, LAYERS - 1) as l:
                dve.wait_ge(agg_zeroed, l * NG + 2)
                carry_wait(dve)
                pipeline(dve, l, msg_ahead, msg_cycle, msg_end, msg_front, settle=settled(dve, M, visits_b),
                         steps=[lambda j: update_step(l, j)])
            dve.wait_ge(agg_zeroed, (LAYERS - 1) * NG + 2)
            pipeline(dve, LAYERS - 1, msg_ahead, msg_cycle, msg_end, msg_front, settle=settled(dve, M, visits_b),
                     steps=[norm_step, None, lambda j: self_step(0, j)])

            def rel_ahead(n, m, q, c, win):
                build_first(R, c, n, q)

            def rel_cycle(n, m, q, c, win):
                rest = pre[q][:, :].rearrange("p (u d) -> p u d", d=D)
                w0, w1 = win[0]
                dve.wait_ge(R["hi_done"], n + 1)
                dve.wait_ge(R["lo_done"], n + 1)
                nc.vector.tensor_tensor(rest, gath[:, ds((c % BUFFERS) * TILES, TILES), :], m3[q][:, :, 0:D],
                                        ALU.subtract).then_inc(R["rest_done"], 1)
                if -1 in win:
                    add_first(R, visits_r, n - 1, 1 - q, win[-1][0])
                dve.wait_ge(R["mid_done"], n + 1)
                nc.vector.tensor_tensor(m3[q][:, :, 2 * D:], rest, m3[q][:, :, D:2 * D],
                                        ALU.subtract).then_inc(R["lo_done"], 1)
                add_extra(R, visits_r, c, n, q, w0, w1)

            def rel_end(n, m, q, c, win):
                add_first(R, visits_r, n, q, win[0][0])

            for r in range(RLAYERS - 1):
                dve.wait_ge(self_added, NG * (r + 1))
                pipeline(dve, r, rel_ahead, rel_cycle, rel_end, settle=settled(dve, R, visits_r),
                         steps=[stage_step, lambda j: self_step(r + 1, j)])
            dve.wait_ge(self_added, NG * RLAYERS)
            pipeline(dve, RLAYERS - 1, rel_ahead, rel_cycle, rel_end, settle=settled(dve, R, visits_r),
                     steps=[last_step])


def layouts(x, src, dst, edge_attr_16, edge_type_8, **rest):
    import numpy as np
    n, e = x.shape[0], len(src)
    rows = -(-n // (P * GROUP)) * (P * GROUP)
    if rows == n:
        rows += P * GROUP
    edges = -(-e // (BUFFERS * CHUNK)) * (BUFFERS * CHUNK)

    def fill(a, length, value):
        to = np.full((length, *a.shape[1:]), value, a.dtype)
        to[:len(a)] = a
        return to

    xp = fill(np.asarray(x), rows, 0)
    s, d, t = (fill(np.asarray(a), edges, v) for a, v in ((src, 0), (dst, n), (edge_type_8, 0)))
    attr = fill(np.asarray(edge_attr_16), edges, 0)
    cols = [np.ascontiguousarray(a.reshape(-1, P).T) for a in (s, d, t)]
    arrays = {"xT": np.ascontiguousarray(xp.T), "x_rows": xp, "src": cols[0], "dst": cols[1], "etype": cols[2],
              "dst_rows": d.reshape(-1, CHUNK),
              "edge_attr": np.ascontiguousarray(attr.reshape(-1, TILES, P, attr.shape[1]).transpose(0, 1, 3, 2)
                                           .reshape(edges // CHUNK, -1, P))}
    for k in ("msg_w", "msg_b", "upd_w", "upd_b"):
        arrays[k] = np.ascontiguousarray(rest["L0_gnn_" + k])
    for r in "12":
        for k in ("bases", "coef", "wself", "bias"):
            arrays[k + r] = np.ascontiguousarray(rest["L1_gnn_" + k + r])
    return arrays


def kernel(**inputs):
    import numpy as np
    import concourse.bacc as bacc
    from concourse.bass_utils import run_bass_kernel_spmd

    arrays = layouts(**inputs)
    nc = bacc.Bacc("TRN2", target_bir_lowering=False, num_devices=1)
    args = [nc.dram_tensor("in_" + k, a.shape, mybir.dt.from_np(a.dtype), kind="ExternalInput").ap()
            for k, a in arrays.items()]
    out = nc.dram_tensor("out", list(arrays["x_rows"].shape), F32, kind="ExternalOutput").ap()
    gnn_kernel(nc, *args, out, len(inputs["src"]))
    r = run_bass_kernel_spmd(nc, [{"in_" + k: a for k, a in arrays.items()}], core_ids=[0])
    return r.results[0]["out"][:len(inputs["x"])]
```
